# Optimizing a Trainium2 kernel written in Bass

```python
import numpy as np
import jax
import jax.numpy as jnp

def _softmax(x, axis=-1):
    return jax.nn.softmax(x, axis=axis)

def _gelu(x):
    return jax.nn.gelu(x, approximate=True)

def _silu(x):
    return jax.nn.silu(x)

def _sigmoid(x):
    return jax.nn.sigmoid(x)

def _layernorm(x, axis=-1, eps=1e-05):
    m = jnp.mean(x, axis=axis, keepdims=True)
    v = jnp.var(x, axis=axis, keepdims=True)
    return (x - m) / jnp.sqrt(v + eps)

def _scatter_add(tgt, idx, src, axis=0):
    return tgt.at[idx].add(src)

def _segment_sum(src, seg, n):
    return jax.ops.segment_sum(src, seg, n)
kernel_name = 'mk_vit_tower_cls_d1_tok_img256_r4_bee4b2'

def setup_inputs(seed: int=0):
    np.random.seed(seed)
    _w = jnp.asarray

    def _rec_inputs():
        import jax
        import jax.numpy as jnp
        _rk = jax.random.key(seed)
        x = 9.04603e-05 + 1.00016 * jax.random.normal(jax.random.fold_in(_rk, 1), (16, 1, 224, 224), jnp.float32)
        cls_tok = 0.02 * jax.random.normal(jax.random.fold_in(_rk, 5), (1, 1, 64), jnp.float32)
        return (x, cls_tok)
    x, cls_tok = _rec_inputs()

    def _L0_tok_setup():
        import jax, jax.numpy as jnp
        import numpy as np
        WS = 7
        H = W = 56
        C = 64
        NH = 8
        HD = C // NH
        SCALE = HD ** (-0.5)
        SHIFT = WS // 2
        N = WS * WS

        def _rel_pos_index():
            coords = np.stack(np.meshgrid(np.arange(WS), np.arange(WS), indexing='ij'))
            cf = coords.reshape(2, -1)
            rel = (cf[:, :, None] - cf[:, None, :]).transpose(1, 2, 0).copy()
            rel[..., 0] += WS - 1
            rel[..., 1] += WS - 1
            rel[..., 0] *= 2 * WS - 1
            return jnp.array(rel.sum(-1))

        def _attn_mask():
            img = np.zeros((H, W), np.int32)
            cnt = 0
            for h in (slice(0, -WS), slice(-WS, -SHIFT), slice(-SHIFT, None)):
                for w in (slice(0, -WS), slice(-WS, -SHIFT), slice(-SHIFT, None)):
                    cnt += 1
                    img[h, w] = cnt
            mw = img.reshape(H // WS, WS, W // WS, WS).transpose(0, 2, 1, 3).reshape(-1, N)
            diff = mw[:, None, :] - mw[:, :, None]
            return jnp.array(np.where(diff != 0, -100.0, 0.0).astype(np.float32))

        def _layernorm(x, g, b):
            m = x.mean(-1, keepdims=True)
            v = ((x - m) ** 2).mean(-1, keepdims=True)
            return (x - m) * jax.lax.rsqrt(v + 1e-05) * g + b

        def _window_partition(x):
            B = x.shape[0]
            x = x.reshape(B, H // WS, WS, W // WS, WS, C).transpose(0, 1, 3, 2, 4, 5)
            return x.reshape(-1, N, C)

        def _window_reverse(xw, B):
            x = xw.reshape(B, H // WS, W // WS, WS, WS, C).transpose(0, 1, 3, 2, 4, 5)
            return x.reshape(B, H, W, C)

        def _swin_block(x, p, shift, rpi, amask):
            B = x.shape[0]
            shortcut = x
            h = _layernorm(x, p['n1g'], p['n1b']).reshape(B, H, W, C)
            if shift > 0:
                h = jnp.roll(h, (-shift, -shift), axis=(1, 2))
            xw = _window_partition(h)
            B_ = xw.shape[0]
            qkv = (xw @ p['qkv_w'].T + p['qkv_b']).reshape(B_, N, 3, NH, HD).transpose(2, 0, 3, 1, 4)
            q, k, v = (qkv[0], qkv[1], qkv[2])
            attn = jnp.einsum('bhnd,bhmd->bhnm', q * SCALE, k)
            attn = attn + p['rpb'][rpi].transpose(2, 0, 1)[None]
            if shift > 0:
                nW = amask.shape[0]
                attn = attn.reshape(B_ // nW, nW, NH, N, N) + amask[None, :, None]
                attn = attn.reshape(B_, NH, N, N)
            attn = jax.nn.softmax(attn, axis=-1)
            o = jnp.einsum('bhnm,bhmd->bhnd', attn, v).transpose(0, 2, 1, 3).reshape(B_, N, C)
            o = o @ p['proj_w'].T + p['proj_b']
            h = _window_reverse(o, B)
            if shift > 0:
                h = jnp.roll(h, (shift, shift), axis=(1, 2))
            x = shortcut + h.reshape(B, H * W, C)
            y = _layernorm(x, p['n2g'], p['n2b'])
            y = jax.nn.gelu(y @ p['w1'].T + p['b1'], approximate=False)
            return x + y @ p['w2'].T + p['b2']
        key = jax.random.key(seed)
        ks = jax.random.split(key, 8)
        s = 0.02
        return {'x': jax.random.normal(ks[0], (16, 1, 224, 224), jnp.float32), 'pe_w': jax.random.normal(ks[1], (C, 1, 4, 4), jnp.float32) * s, 'pe_b': jnp.zeros((C,), jnp.float32), 'pe_ng': jnp.ones((C,), jnp.float32), 'pe_nb': jnp.zeros((C,), jnp.float32), 'n1g': jnp.ones((2, C), jnp.float32), 'n1b': jnp.zeros((2, C), jnp.float32), 'qkv_w': jax.random.normal(ks[2], (2, 3 * C, C), jnp.float32) * s, 'qkv_b': jnp.zeros((2, 3 * C), jnp.float32), 'rpb': jax.random.normal(ks[3], (2, (2 * WS - 1) ** 2, NH), jnp.float32) * s, 'proj_w': jax.random.normal(ks[4], (2, C, C), jnp.float32) * s, 'proj_b': jnp.zeros((2, C), jnp.float32), 'n2g': jnp.ones((2, C), jnp.float32), 'n2b': jnp.zeros((2, C), jnp.float32), 'w1': jax.random.normal(ks[5], (2, 4 * C, C), jnp.float32) * s, 'b1': jnp.zeros((2, 4 * C), jnp.float32), 'w2': jax.random.normal(ks[6], (2, C, 4 * C), jnp.float32) * s, 'b2': jnp.zeros((2, C), jnp.float32)}
    _L0_tok_all = _L0_tok_setup()
    _L0_tok_in = {k: v for k, v in _L0_tok_all.items() if k in ('pe_w', 'pe_b', 'pe_ng', 'pe_nb', 'n1g', 'n1b', 'qkv_w', 'qkv_b', 'rpb', 'proj_w', 'proj_b', 'n2g', 'n2b', 'w1', 'b1', 'w2', 'b2')}
    del _L0_tok_all

    def _L0_attn_setup():
        import jax, jax.numpy as jnp
        import numpy as np
        D, H, L, S_MAX = (64, 8, 4, 1024)
        DH = D // H
        FF = 4 * D
        B, S = (16, 1024)

        def _pe(seq_len, d):
            pos = jnp.arange(seq_len, dtype=jnp.float32)[:, None]
            div = jnp.exp(jnp.arange(0, d, 2, dtype=jnp.float32) * (-jnp.log(10000.0) / d))
            pe = jnp.zeros((seq_len, d), dtype=jnp.float32)
            pe = pe.at[:, 0::2].set(jnp.sin(pos * div))
            pe = pe.at[:, 1::2].set(jnp.cos(pos * div))
            return pe

        def _ln(x, g, b, eps=1e-05):
            mu = jnp.mean(x, axis=-1, keepdims=True)
            var = jnp.var(x, axis=-1, keepdims=True)
            return (x - mu) * jax.lax.rsqrt(var + eps) * g + b
        key = jax.random.key(seed)
        ks = jax.random.split(key, 12)
        s = 0.02
        return {'x': jax.random.normal(ks[0], (B, S, D), dtype=jnp.float32), 'Wq': jax.random.normal(ks[1], (L, D, D), dtype=jnp.float32) * s, 'Wk': jax.random.normal(ks[2], (L, D, D), dtype=jnp.float32) * s, 'Wv': jax.random.normal(ks[3], (L, D, D), dtype=jnp.float32) * s, 'Wo': jax.random.normal(ks[4], (L, D, D), dtype=jnp.float32) * s, 'bo': jnp.zeros((L, D), dtype=jnp.float32), 'g1': jnp.ones((L, D), dtype=jnp.float32), 'b1': jnp.zeros((L, D), dtype=jnp.float32), 'W1': jax.random.normal(ks[5], (L, D, FF), dtype=jnp.float32) * s, 'bf1': jnp.zeros((L, FF), dtype=jnp.float32), 'W2': jax.random.normal(ks[6], (L, FF, D), dtype=jnp.float32) * s, 'bf2': jnp.zeros((L, D), dtype=jnp.float32), 'g2': jnp.ones((L, D), dtype=jnp.float32), 'b2': jnp.zeros((L, D), dtype=jnp.float32)}
    _L0_attn_all = _L0_attn_setup()
    _L0_attn_in = {k: v for k, v in _L0_attn_all.items() if k in ('Wq', 'Wk', 'Wv', 'Wo', 'bo', 'g1', 'b1', 'W1', 'bf1', 'W2', 'bf2', 'g2', 'b2')}
    del _L0_attn_all

    def _L0_ffn_setup():
        import jax, jax.numpy as jnp
        import numpy as np
        E = 8
        K = 2
        D = 64
        H = 128
        DOUT = 64
        EPS = 1e-05
        key = jax.random.key(seed)
        ks = jax.random.split(key, 9)
        s = 0.02
        return {'x': jax.random.normal(ks[0], (4, 2048, D), jnp.float32), 'gamma': 1.0 + 0.05 * jax.random.normal(ks[1], (D,), jnp.float32), 'beta': 0.05 * jax.random.normal(ks[2], (D,), jnp.float32), 'Wr': 0.01 * jax.random.normal(ks[3], (D, E), jnp.float32), 'br': jnp.zeros((E,), jnp.float32), 'W1': s * jax.random.normal(ks[4], (E, D, H), jnp.float32), 'b1': s * jax.random.normal(ks[5], (E, H), jnp.float32), 'W2': s * jax.random.normal(ks[6], (E, H, DOUT), jnp.float32), 'b2': s * jax.random.normal(ks[7], (E, DOUT), jnp.float32)}
    _L0_ffn_all = _L0_ffn_setup()
    _L0_ffn_in = {k: v for k, v in _L0_ffn_all.items() if k in ('gamma', 'beta', 'Wr', 'br', 'W1', 'b1', 'W2', 'b2')}
    del _L0_ffn_all
    return {'x': x, 'cls_tok': cls_tok, 'L0_tok_pe_w': _L0_tok_in['pe_w'], 'L0_tok_pe_b': _L0_tok_in['pe_b'], 'L0_tok_pe_ng': _L0_tok_in['pe_ng'], 'L0_tok_pe_nb': _L0_tok_in['pe_nb'], 'L0_tok_n1g': _L0_tok_in['n1g'], 'L0_tok_n1b': _L0_tok_in['n1b'], 'L0_tok_qkv_w': _L0_tok_in['qkv_w'], 'L0_tok_qkv_b': _L0_tok_in['qkv_b'], 'L0_tok_rpb': _L0_tok_in['rpb'], 'L0_tok_proj_w': _L0_tok_in['proj_w'], 'L0_tok_proj_b': _L0_tok_in['proj_b'], 'L0_tok_n2g': _L0_tok_in['n2g'], 'L0_tok_n2b': _L0_tok_in['n2b'], 'L0_tok_w1': _L0_tok_in['w1'], 'L0_tok_b1': _L0_tok_in['b1'], 'L0_tok_w2': _L0_tok_in['w2'], 'L0_tok_b2': _L0_tok_in['b2'], 'L0_attn_Wq': _L0_attn_in['Wq'], 'L0_attn_Wk': _L0_attn_in['Wk'], 'L0_attn_Wv': _L0_attn_in['Wv'], 'L0_attn_Wo': _L0_attn_in['Wo'], 'L0_attn_bo': _L0_attn_in['bo'], 'L0_attn_g1': _L0_attn_in['g1'], 'L0_attn_b1': _L0_attn_in['b1'], 'L0_attn_W1': _L0_attn_in['W1'], 'L0_attn_bf1': _L0_attn_in['bf1'], 'L0_attn_W2': _L0_attn_in['W2'], 'L0_attn_bf2': _L0_attn_in['bf2'], 'L0_attn_g2': _L0_attn_in['g2'], 'L0_attn_b2': _L0_attn_in['b2'], 'L0_ffn_gamma': _L0_ffn_in['gamma'], 'L0_ffn_beta': _L0_ffn_in['beta'], 'L0_ffn_Wr': _L0_ffn_in['Wr'], 'L0_ffn_br': _L0_ffn_in['br'], 'L0_ffn_W1': _L0_ffn_in['W1'], 'L0_ffn_b1': _L0_ffn_in['b1'], 'L0_ffn_W2': _L0_ffn_in['W2'], 'L0_ffn_b2': _L0_ffn_in['b2']}

def reference(x, cls_tok, L0_tok_pe_w, L0_tok_pe_b, L0_tok_pe_ng, L0_tok_pe_nb, L0_tok_n1g, L0_tok_n1b, L0_tok_qkv_w, L0_tok_qkv_b, L0_tok_rpb, L0_tok_proj_w, L0_tok_proj_b, L0_tok_n2g, L0_tok_n2b, L0_tok_w1, L0_tok_b1, L0_tok_w2, L0_tok_b2, L0_attn_Wq, L0_attn_Wk, L0_attn_Wv, L0_attn_Wo, L0_attn_bo, L0_attn_g1, L0_attn_b1, L0_attn_W1, L0_attn_bf1, L0_attn_W2, L0_attn_bf2, L0_attn_g2, L0_attn_b2, L0_ffn_gamma, L0_ffn_beta, L0_ffn_Wr, L0_ffn_br, L0_ffn_W1, L0_ffn_b1, L0_ffn_W2, L0_ffn_b2):
    import jax
    import jax.numpy as jnp

    def _L0_tok_ref(x, pe_w, pe_b, pe_ng, pe_nb, n1g, n1b, qkv_w, qkv_b, rpb, proj_w, proj_b, n2g, n2b, w1, b1, w2, b2):
        import jax, jax.numpy as jnp
        import numpy as np
        WS = 7
        H = W = 56
        C = 64
        NH = 8
        HD = C // NH
        SCALE = HD ** (-0.5)
        SHIFT = WS // 2
        N = WS * WS

        def _rel_pos_index():
            coords = np.stack(np.meshgrid(np.arange(WS), np.arange(WS), indexing='ij'))
            cf = coords.reshape(2, -1)
            rel = (cf[:, :, None] - cf[:, None, :]).transpose(1, 2, 0).copy()
            rel[..., 0] += WS - 1
            rel[..., 1] += WS - 1
            rel[..., 0] *= 2 * WS - 1
            return jnp.array(rel.sum(-1))

        def _attn_mask():
            img = np.zeros((H, W), np.int32)
            cnt = 0
            for h in (slice(0, -WS), slice(-WS, -SHIFT), slice(-SHIFT, None)):
                for w in (slice(0, -WS), slice(-WS, -SHIFT), slice(-SHIFT, None)):
                    cnt += 1
                    img[h, w] = cnt
            mw = img.reshape(H // WS, WS, W // WS, WS).transpose(0, 2, 1, 3).reshape(-1, N)
            diff = mw[:, None, :] - mw[:, :, None]
            return jnp.array(np.where(diff != 0, -100.0, 0.0).astype(np.float32))

        def _layernorm(x, g, b):
            m = x.mean(-1, keepdims=True)
            v = ((x - m) ** 2).mean(-1, keepdims=True)
            return (x - m) * jax.lax.rsqrt(v + 1e-05) * g + b

        def _window_partition(x):
            B = x.shape[0]
            x = x.reshape(B, H // WS, WS, W // WS, WS, C).transpose(0, 1, 3, 2, 4, 5)
            return x.reshape(-1, N, C)

        def _window_reverse(xw, B):
            x = xw.reshape(B, H // WS, W // WS, WS, WS, C).transpose(0, 1, 3, 2, 4, 5)
            return x.reshape(B, H, W, C)

        def _swin_block(x, p, shift, rpi, amask):
            B = x.shape[0]
            shortcut = x
            h = _layernorm(x, p['n1g'], p['n1b']).reshape(B, H, W, C)
            if shift > 0:
                h = jnp.roll(h, (-shift, -shift), axis=(1, 2))
            xw = _window_partition(h)
            B_ = xw.shape[0]
            qkv = (xw @ p['qkv_w'].T + p['qkv_b']).reshape(B_, N, 3, NH, HD).transpose(2, 0, 3, 1, 4)
            q, k, v = (qkv[0], qkv[1], qkv[2])
            attn = jnp.einsum('bhnd,bhmd->bhnm', q * SCALE, k)
            attn = attn + p['rpb'][rpi].transpose(2, 0, 1)[None]
            if shift > 0:
                nW = amask.shape[0]
                attn = attn.reshape(B_ // nW, nW, NH, N, N) + amask[None, :, None]
                attn = attn.reshape(B_, NH, N, N)
            attn = jax.nn.softmax(attn, axis=-1)
            o = jnp.einsum('bhnm,bhmd->bhnd', attn, v).transpose(0, 2, 1, 3).reshape(B_, N, C)
            o = o @ p['proj_w'].T + p['proj_b']
            h = _window_reverse(o, B)
            if shift > 0:
                h = jnp.roll(h, (shift, shift), axis=(1, 2))
            x = shortcut + h.reshape(B, H * W, C)
            y = _layernorm(x, p['n2g'], p['n2b'])
            y = jax.nn.gelu(y @ p['w1'].T + p['b1'], approximate=False)
            return x + y @ p['w2'].T + p['b2']
        B = x.shape[0]
        h = jax.lax.conv_general_dilated(x, pe_w, (4, 4), 'VALID', dimension_numbers=('NCHW', 'OIHW', 'NCHW'))
        h = h + pe_b[None, :, None, None]
        t = h.reshape(B, C, H * W).transpose(0, 2, 1)
        t = _layernorm(t, pe_ng, pe_nb)
        rpi = _rel_pos_index()
        amask = _attn_mask()
        for i, shift in enumerate((0, SHIFT)):
            p = {'n1g': n1g[i], 'n1b': n1b[i], 'qkv_w': qkv_w[i], 'qkv_b': qkv_b[i], 'rpb': rpb[i], 'proj_w': proj_w[i], 'proj_b': proj_b[i], 'n2g': n2g[i], 'n2b': n2b[i], 'w1': w1[i], 'b1': b1[i], 'w2': w2[i], 'b2': b2[i]}
            t = _swin_block(t, p, shift, rpi, amask)
        return t

    def _L0_attn_ref(x, Wq, Wk, Wv, Wo, bo, g1, b1, W1, bf1, W2, bf2, g2, b2):
        import jax, jax.numpy as jnp
        import numpy as np
        D, H, L, S_MAX = (64, 8, 4, 1024)
        DH = D // H
        FF = 4 * D
        B, S = (16, 1024)

        def _pe(seq_len, d):
            pos = jnp.arange(seq_len, dtype=jnp.float32)[:, None]
            div = jnp.exp(jnp.arange(0, d, 2, dtype=jnp.float32) * (-jnp.log(10000.0) / d))
            pe = jnp.zeros((seq_len, d), dtype=jnp.float32)
            pe = pe.at[:, 0::2].set(jnp.sin(pos * div))
            pe = pe.at[:, 1::2].set(jnp.cos(pos * div))
            return pe

        def _ln(x, g, b, eps=1e-05):
            mu = jnp.mean(x, axis=-1, keepdims=True)
            var = jnp.var(x, axis=-1, keepdims=True)
            return (x - mu) * jax.lax.rsqrt(var + eps) * g + b
        b, s, d = x.shape
        x = x + _pe(s, d)[None, :, :]
        scale = DH ** (-0.5)
        for l in range(L):
            h = _ln(x, g1[l], b1[l])
            q = (h @ Wq[l]).reshape(b, s, H, DH).transpose(0, 2, 1, 3)
            k = (h @ Wk[l]).reshape(b, s, H, DH).transpose(0, 2, 1, 3)
            v = (h @ Wv[l]).reshape(b, s, H, DH).transpose(0, 2, 1, 3)
            q = jax.nn.softmax(q, axis=-1) * scale
            k = jax.nn.softmax(k, axis=-2)
            ctx = jnp.einsum('bhnd,bhne->bhde', k, v)
            attn = jnp.einsum('bhnd,bhde->bhne', q, ctx)
            attn = attn.transpose(0, 2, 1, 3).reshape(b, s, d)
            x = x + attn @ Wo[l] + bo[l]
            h = _ln(x, g2[l], b2[l])
            x = x + jax.nn.gelu(h @ W1[l] + bf1[l], approximate=False) @ W2[l] + bf2[l]
        return x

    def _L0_ffn_ref(x, gamma, beta, Wr, br, W1, b1, W2, b2):
        import jax, jax.numpy as jnp
        import numpy as np
        E = 8
        K = 2
        D = 64
        H = 128
        DOUT = 64
        EPS = 1e-05
        mu = jnp.mean(x, axis=-1, keepdims=True)
        var = jnp.mean(jnp.square(x - mu), axis=-1, keepdims=True)
        xn = (x - mu) * jax.lax.rsqrt(var + EPS) * gamma + beta
        logits = jnp.einsum('bsd,de->bse', xn, Wr) + br
        top_vals, top_idx = jax.lax.top_k(logits, K)
        w = jax.nn.softmax(top_vals, axis=-1)
        w_full = jnp.einsum('bsk,bske->bse', w, jax.nn.one_hot(top_idx, E, dtype=w.dtype))
        y = jnp.zeros(x.shape[:-1] + (DOUT,), x.dtype)
        for e in range(E):
            h = jax.nn.gelu(jnp.einsum('bsd,dh->bsh', xn, W1[e]) + b1[e], approximate=False)
            y_e = jnp.einsum('bsh,hd->bsd', h, W2[e]) + b2[e]
            y = y + y_e * w_full[..., e, None]
        return y
    h = _L0_tok_ref(x, L0_tok_pe_w, L0_tok_pe_b, L0_tok_pe_ng, L0_tok_pe_nb, L0_tok_n1g, L0_tok_n1b, L0_tok_qkv_w, L0_tok_qkv_b, L0_tok_rpb, L0_tok_proj_w, L0_tok_proj_b, L0_tok_n2g, L0_tok_n2b, L0_tok_w1, L0_tok_b1, L0_tok_w2, L0_tok_b2)
    h = jnp.concatenate([jnp.broadcast_to(cls_tok, (h.shape[0], 1, h.shape[2])), h], axis=1)
    h = h + _L0_attn_ref(_layernorm(h, axis=-1), L0_attn_Wq, L0_attn_Wk, L0_attn_Wv, L0_attn_Wo, L0_attn_bo, L0_attn_g1, L0_attn_b1, L0_attn_W1, L0_attn_bf1, L0_attn_W2, L0_attn_bf2, L0_attn_g2, L0_attn_b2)
    h = h + _L0_ffn_ref(_layernorm(h, axis=-1), L0_ffn_gamma, L0_ffn_beta, L0_ffn_Wr, L0_ffn_br, L0_ffn_W1, L0_ffn_b1, L0_ffn_W2, L0_ffn_b2)
    return h

_drawn_inputs = setup_inputs


def setup_inputs(seed=0):
    import zlib

    import numpy as np

    out = dict(_drawn_inputs(seed))
    spreads = {'L0_tok_pe_b': (0.0, 0.1),
     'L0_tok_pe_ng': (1.0, 0.2),
     'L0_tok_pe_nb': (0.0, 0.1),
     'L0_tok_n1g': (1.0, 0.6),
     'L0_tok_n1b': (0.0, 0.8),
     'L0_tok_qkv_b': (0.0, 0.462),
     'L0_tok_proj_b': (0.0, 0.1),
     'L0_tok_n2g': (1.0, 0.6),
     'L0_tok_n2b': (0.0, 0.8),
     'L0_tok_b1': (0.0, 0.417),
     'L0_tok_b2': (0.0, 0.1),
     'L0_attn_bo': (0.0, 0.1),
     'L0_attn_g1': (1.0, 0.6),
     'L0_attn_b1': (0.0, 0.8),
     'L0_attn_bf1': (0.0, 0.559),
     'L0_attn_bf2': (0.0, 0.1),
     'L0_attn_g2': (1.0, 0.6),
     'L0_attn_b2': (0.0, 0.8),
     'L0_ffn_br': (0.0, 0.8)}
    factors = {'cls_tok': 200.0,
     'L0_tok_rpb': 192.375,
     'L0_attn_Wq': 8.0,
     'L0_attn_Wk': 8.0,
     'L0_attn_Wv': 8.0,
     'L0_attn_Wo': 8.0,
     'L0_ffn_gamma': 8.0,
     'L0_ffn_beta': 8.0,
     'L0_ffn_Wr': 8.0,
     'L0_ffn_W1': 8.0,
     'L0_ffn_b1': 31.251,
     'L0_ffn_W2': 8.0,
     'L0_ffn_b2': 41.911}
    for name, (base, spread) in spreads.items():
        noise = np.random.default_rng([zlib.crc32(name.encode()), seed]).standard_normal(out[name].shape)
        drawn = base * np.exp(spread * noise) if base else spread * noise
        out[name] = jnp.asarray(drawn.astype(out[name].dtype))
    for name, factor in factors.items():
        out[name] = (out[name] * factor).astype(out[name].dtype)
    return out
```

```python
from contextlib import ExitStack

import numpy as np

import concourse.bass as bass
from concourse import mybir

F32 = mybir.dt.float32
BF16 = mybir.dt.bfloat16
F32R = mybir.dt.float32r
ALU = mybir.AluOpType
ACT = mybir.ActivationFunctionType
AX = mybir.AxisListType

B, IMG, PATCH = 16, 224, 4
GRID = IMG // PATCH
TOK = GRID * GRID
C, HEADS, HD = 64, 8, 8
PAIRS = B // 2
P = 128
WS, SHIFT = 7, 3
WIN = WS * WS
NW = GRID // WS
STRIP = WS * GRID
SEQ = TOK + 1
CH = 8
TT = 99
TPC = 4
CW = TT * TPC
SEQP = CH * CW
NT = CH * TPC
BASE = SHIFT * GRID
PSTR = BASE + SEQP
FF = 4 * C
EXP, TOPK_BIG = 8, -1.0e38
EPS = 1e-5
QSCALE = float(HD) ** -0.5
LAST = SEQ - (CH - 1) * CW

TW = {"q": 0, "k": 128, "v0": 256, "v1": 384, "p": 512, "w1": 640, "w2": 640 + FF}
TW_N = TW["w2"] + 2 * C
TV = {"g1": 0, "b1": 1, "q": 2, "k": 3, "v": 4, "p": 5, "g2": 6, "b2": 7, "f1": 8, "f2": 10}
TV_N = 11
LW = {"k": 0, "q": 128, "v": 256, "o": 384, "w1": 512, "w2": 512 + FF}
LW_N = LW["w2"] + 2 * C
LV = {"g1": 0, "b1": 1, "o": 2, "g2": 3, "b2": 4, "f1": 5, "f2": 7}
LV_N = 8
MW = {"r": 0, "w2": 2 * EXP}
MW_N = MW["w2"] + EXP * C
MV = {"g": 0, "b": 1, "f1": 2}
MV_N = 2 + EXP


def vit_tower(nc, t, out):
    ctx = ExitStack()
    with ctx:
        def sb(name, shape, dt=F32):
            return ctx.enter_context(nc.sbuf_tensor(name, shape, dt))

        def sem(name):
            return ctx.enter_context(nc.semaphore(name))

        X = sb("X", [P, PAIRS * PSTR])
        XN = sb("XN", [P, SEQP + 32])
        KS = sb("KS", [P, SEQP])
        sq = sb("sq", [P, 2, CW])
        rs = sb("rs", [P, 2, CW])
        hid = sb("hid", [P, 8, CW])
        xs = sb("xs", [P, 2, 2, CW], F32R)
        w1p = sb("w1p", [P, 2, FF], F32R)
        eps = sb("eps", [P, 1])
        junk = sb("junk", [P, 1])
        centre = sb("centre", [P, P])
        mean = sb("mean", [P, P])
        ident = sb("ident", [P, P])
        bdmask = sb("bdmask", [P, P])
        banks = [ctx.enter_context(nc.psum_tensor(f"bank{i}", [P, 512], F32)) for i in range(8)]

        h_dram = nc.dram_tensor("h_spill", (PAIRS, P, SEQP), F32).ap()

        def xcols(p, a, n):
            return X[:, bass.ds(p * PSTR + a, n)]

        s_load = sem("s_load")
        s_const = sem("s_const")
        s_arrived = sem("dma_arrived")
        LOADED = 16 * (4 + PAIRS)
        with nc.Block() as block:
            @block.sync
            def _(sp):
                sp.dma_start(centre[:, :], t["centre"]).then_inc(s_load, 16)
                sp.dma_start(mean[:, :], t["mean"]).then_inc(s_load, 16)
                sp.dma_start(ident[:, :], t["ident"]).then_inc(s_load, 16)
                sp.dma_start(bdmask[:, :], t["bdmask"]).then_inc(s_load, 16)
                sp.wait_ge(s_const, 4)
                for p in range(PAIRS):
                    sp.dma_start(X[:, p * PSTR + BASE + TOK:p * PSTR + BASE + TOK + 1], t["cls"],
                                 ).then_inc(s_load, 16)
                sp.wait_ge(s_load, LOADED)

            @block.vector
            def _(dve):
                dve.memset(eps[:, :], EPS).then_inc(s_const, 1)
                dve.memset(XN[:, :], 0.0).then_inc(s_const, 1)
                dve.memset(junk[:, :], 1.0).then_inc(s_const, 1)
                dve.memset(X[:, :].rearrange("p (a n) -> p a n", a=PAIRS)[:, :, BASE + TOK:], 0.0)\
                    .then_inc(s_const, 1)

        s_xc = sem("ln_centred")
        s_sq = sem("ln_squared")
        s_var = sem("ln_variance")
        s_rs = sem("ln_rstd")
        s_xn = sem("ln_normalised")
        s_af = sem("ln_affine")

        def layer_norm(it, width, pieces, dst, shape, gb=None, plain=None):
            def done(k):
                return it * CH + k + 1

            with nc.Block() as block:
                @block.tensor
                def _(pe):
                    def variance(k):
                        pe.wait_ge(s_sq, done(k))
                        if k >= 2:
                            pe.wait_ge(s_rs, done(k - 2))
                        pe.matmul(banks[4 + k % 2][:, 0:width], mean[:, :], sq[:, k % 2, 0:width],
                                  start=True, stop=True).then_inc(s_var, 1)

                    for k in range(CH):
                        if k >= 4:
                            pe.wait_ge(s_xn, done(k - 4))
                        parts = pieces(k, banks[k % 4][:, 0:width])
                        for n, (o, src) in enumerate(parts):
                            last = pe.matmul(o, centre[:, :], src, start=True, stop=True)
                        last.then_inc(s_xc, 1)
                        if k:
                            variance(k - 1)
                    variance(CH - 1)

                @block.scalar
                def _(act):
                    act.activation(junk[:, :], junk[:, :], ACT.Abs_reciprocal_sqrt)

                    def rstd(k):
                        act.wait_ge(s_var, done(k))
                        if k >= 2:
                            act.wait_ge(s_xn, done(k - 2))
                        act.activation(rs[:, k % 2, 0:width], banks[4 + k % 2][:, 0:width],
                                       ACT.Abs_reciprocal_sqrt, bias=eps[:, :]).then_inc(s_rs, 1)

                    for k in range(CH):
                        act.wait_ge(s_xc, done(k))
                        if k >= 2:
                            act.wait_ge(s_var, done(k - 2))
                        act.activation(sq[:, k % 2, 0:width], banks[k % 4][:, 0:width], ACT.Square)\
                            .then_inc(s_sq, 1)
                        if k:
                            rstd(k - 1)
                    rstd(CH - 1)

                @block.vector
                def _(dve):
                    def affine(k):
                        dve.wait_ge(s_xn, done(k))
                        v = (plain or dst)(k)
                        dve.tensor_scalar(v, v, gb[0], gb[1], ALU.mult, ALU.add).then_inc(s_af, 1)

                    for k in range(CH):
                        dve.wait_ge(s_rs, done(k))
                        dve.tensor_tensor(dst(k), shape(banks[k % 4][:, 0:width]), shape(rs[:, k % 2, 0:width]),
                                          ALU.mult).then_inc(s_xn, 1)
                        if k and gb is not None:
                            affine(k - 1)
                    if gb is not None:
                        affine(CH - 1)

        def flat(v):
            return v

        def windows(v):
            return v.rearrange("p (row win c) -> p win row c", row=WS, win=NW)

        s_hi = sem("split_high")
        s_lo = sem("split_low")

        def split_chunk(dve, it, k, width, used):
            used()
            x = XN[:, k * width:(k + 1) * width]
            for h in range(2):
                r0, r1 = h * C, (h + 1) * C
                last = dve.tensor_copy(xs[r0:r1, k % 2, h, 0:width], x[r0:r1, :])
            last.then_inc(s_hi, 1)
            dve.wait_ge(s_hi, it * CH + k + 1)
            for h in range(2):
                r0, r1 = h * C, (h + 1) * C
                o = xs[C - r0:2 * C - r0, k % 2, h, 0:width]
                last = dve.tensor_tensor(o, x[r0:r1, :], xs[r0:r1, k % 2, h, 0:width].bitcast(F32), ALU.subtract)
            last.then_inc(s_lo, 1)

        def exact(pe, out, wh, wl, moving):
            pe.matmul(out, wh, moving, start=True, stop=False)
            return pe.matmul(out, wl, moving, start=False, stop=True)

        s_w1h = sem("w1_high")
        s_w1l = sem("w1_low")

        def split_weights(dve, n, w):
            dve.tensor_copy(w1p[:, 0, :], w).then_inc(s_w1h, 1)
            dve.wait_ge(s_w1h, n + 1)
            dve.tensor_tensor(w1p[:, 1, :], w, w1p[:, 0, :].bitcast(F32), ALU.subtract).then_inc(s_w1l, 1)

        s_up = sem("ff_up")
        s_ge = sem("ff_gelu")
        s_dn = sem("ff_down")
        s_fr = sem("ff_residual")

        def feed_forward(it, p, width, base, w2, f1, f2):
            def done(n, k):
                return it * (CH * n) + k + 1

            with nc.Block() as block:
                @block.tensor
                def _(pe):
                    def up(k):
                        pe.wait_ge(s_lo, done(1, k))
                        for u in range(4):
                            n = 4 * k + u
                            if n >= 4:
                                pe.wait_ge(s_ge, done(4, n - 4))
                            h, j = divmod(u, 2)
                            exact(pe, banks[u][:, 0:width], w1p[:, 0, j * P:(j + 1) * P],
                                  w1p[:, 1, j * P:(j + 1) * P], xs[:, k % 2, h, 0:width]).then_inc(s_up, 1)

                    def down(k):
                        pe.wait_ge(s_ge, done(4, 4 * k + 3))
                        if k >= 2:
                            pe.wait_ge(s_fr, done(1, k - 2))
                        for j in range(2):
                            for h in range(2):
                                last = pe.matmul(banks[4 + k % 2][h * C:(h + 1) * C, 0:width],
                                                 w2[:, j * C:(j + 1) * C], hid[:, 4 * (k % 2) + 2 * h + j, 0:width],
                                                 start=(j == 0), stop=(j == 1))
                        last.then_inc(s_dn, 1)

                    for k in range(CH):
                        up(k)
                        if k:
                            down(k - 1)
                    down(CH - 1)

                @block.scalar
                def _(act):
                    for k in range(CH):
                        for u in range(4):
                            act.wait_ge(s_up, done(4, 4 * k + u))
                            if k >= 2 and u == 0:
                                act.wait_ge(s_dn, done(1, k - 2))
                            act.activation(hid[:, 4 * (k % 2) + u, 0:width], banks[u][:, 0:width], ACT.Gelu,
                                           bias=f1[:, u % 2:u % 2 + 1]).then_inc(s_ge, 1)

                @block.vector
                def _(dve):
                    def used(k):
                        if k >= 2:
                            dve.wait_ge(s_up, done(4, 4 * (k - 2) + 3))

                    split_chunk(dve, it, 0, width, lambda: None)
                    for k in range(CH + 1):
                        if k + 1 < CH:
                            split_chunk(dve, it, k + 1, width, lambda: used(k + 1))
                        if k:
                            dve.wait_ge(s_dn, done(1, k - 1))
                            x = xcols(p, base + (k - 1) * width, width)
                            dve.scalar_tensor_tensor(x, banks[4 + (k - 1) % 2][:, 0:width], f2, x, ALU.add, ALU.add)\
                                .then_inc(s_fr, 1)

        with ExitStack() as tok:
            def sbt(name, shape, dt=F32):
                return tok.enter_context(nc.sbuf_tensor(name, shape, dt))

            patches = KS[0:2 * PATCH * PATCH, 0:TOK]
            pe_w = sbt("pe_w", [32, P])
            pe_v = sbt("pe_v", [P, 3])
            s_pin = sem("pe_loaded")
            s_pw = sem("pe_weights")
            s_pc = sem("pe_conv")
            s_pe = sem("pe_stored")
            with nc.Block() as block:
                @block.sync
                def _(sp):
                    sp.dma_start(pe_w[:, :], t["pe_w"]).then_inc(s_pw, 16)
                    sp.dma_start(pe_v[:, :], t["pe_v"]).then_inc(s_pw, 16)
                    sp.wait_ge(s_pw, 32)
            with nc.Fori(0, PAIRS) as p:
                with nc.Block() as block:
                    @block.sync
                    def _(sp):
                        sp.dma_start(patches, t["patches"][bass.ds(p, 1), :, :].rearrange("a k n -> k (a n)"))\
                            .then_inc(s_pin, 16)

                    @block.tensor
                    def _(pe):
                        pe.wait_ge(s_pin, p * 16 + 16)
                        for k in range(CH):
                            if k >= 4:
                                pe.wait_ge(s_pe, p * CH + k - 3)
                            pe.matmul(banks[k % 4][:, 0:STRIP], pe_w[:, :], patches[:, k * STRIP:(k + 1) * STRIP],
                                      start=True, stop=True).then_inc(s_pc, 1)

                    @block.scalar
                    def _(act):
                        for k in range(CH):
                            act.wait_ge(s_pc, p * CH + k + 1)
                            act.activation(xcols(p, k * STRIP, STRIP), banks[k % 4][:, 0:STRIP], ACT.Identity,
                                           bias=pe_v[:, 0:1]).then_inc(s_pe, 1)
                layer_norm(p, STRIP, lambda k, o: [(o, xcols(p, k * STRIP, STRIP))],
                           lambda k: xcols(p, k * STRIP, STRIP), flat, (pe_v[:, 1:2], pe_v[:, 2:3]))

            tw = sbt("tw", [P, TW_N])
            tv = sbt("tv", [P, TV_N])
            bias = sbt("bias", [P, 4, HEADS * WIN])
            amask = sbt("amask", [P, 4, WIN])
            headmask = sbt("headmask", [P, HEADS])
            stack = sbt("stack", [P, WIN])
            flat_hid = hid[:, :, :].rearrange("p a n -> p (a n)")
            qbd = KS[:, 0:2 * NW * P].rearrange("p (s a n) -> p s a n", s=2, a=NW)
            ksb = KS[:, 2 * NW * P:2 * NW * P + 2 * STRIP].rearrange("p (s n) -> p s n", s=2)
            kbd = flat_hid[:, 0:4 * STRIP].rearrange("p (s h n) -> p s h n", s=4, h=HEADS)
            probT = flat_hid[:, 4 * STRIP:4 * STRIP + 8 * P].rearrange("p (s a n) -> p s a n", s=2, a=4)
            osb = flat_hid[:, 4 * STRIP + 8 * P:5 * STRIP + 8 * P]
            ssb = sbt("ssb", [P, 3, HEADS, WIN])
            smax = sbt("smax", [P, 3, HEADS])
            prob = sbt("prob", [P, 3, HEADS, C])
            vb = sbt("vb", [P, 8, 2, HEADS, HD + 1])
            rcp = sbt("rcp", [P, 2, HEADS])
            obd = sbt("obd", [P, 2, P])
            psb = sbt("psb", [P, STRIP])
            s_tc = sem("swin_cleared")
            s_tl = sem("swin_loaded")
            s_bt = sem("swin_bias")
            sa = {n: sem("att_" + n) for n in (
                "q", "k", "qev", "kev", "kbd", "v", "s", "add", "max", "sub", "exp", "t", "tev", "vev", "av",
                "rcp", "nrm", "ot", "oev", "pj", "pev")}
            s_res = {n: sem(f"att_residual_{n}") for n in (0, SHIFT)}
            NG = NW * NW

            with nc.Block() as block:
                @block.vector
                def _(dve):
                    for m in (qbd[:, :, :, :], prob[:, :, :, :], obd[:, :, :], bias[:, :, :]):
                        dve.memset(m, 0.0).then_inc(s_tc, 1)
                    dve.memset(vb[:, :, :, :, :], 1.0).then_inc(s_tc, 1)

                @block.gpsimd
                def _(pool):
                    pool.wait_ge(s_tc, 5)
                    v = vb[:, :, :, :, :].rearrange("p a w (j e) d -> p (a w j) e d", e=2)
                    pool.memset(v[0:C, :, 1, :], 0.0).then_inc(s_tc, 1)
                    pool.memset(v[C:P, :, 0, :], 0.0).then_inc(s_tc, 1)

                @block.sync
                def _(sp):
                    sp.dma_start(headmask[:, :], t["headmask"]).then_inc(s_tl, 16)
                    sp.dma_start(stack[:, :], t["stack"]).then_inc(s_tl, 16)
                    sp.wait_ge(s_tl, 32)

            def swin_load(layer):
                with nc.Block() as block:
                    @block.sync
                    def _(sp):
                        sp.dma_start(tw[:, :], t["tok_w"][layer, :, :]).then_inc(s_tl, 16)
                        sp.dma_start(tv[:, :], t["tok_v"][layer, :, :]).then_inc(s_tl, 16)
                        sp.dma_start(amask[:, :, :], t["amask"][layer, :, :, :]).then_inc(s_tl, 16)
                        for n in range(WIN):
                            ni, nj = divmod(n, WS)
                            src = t["rpb_rev"][layer, :, WS - 1 - ni:2 * WS - 1 - ni, WS - 1 - nj:2 * WS - 1 - nj]
                            dst = bias[n:n + 1, 0, :].rearrange("p (h a b) -> p h a b", h=HEADS, a=WS)
                            sp.dma_start(dst, src.unsqueeze(0)).then_inc(s_tl, 16)
                        first = 32 + (layer + 1) * 16 * (3 + WIN) + layer * 16
                        sp.wait_ge(s_tl, first)
                        sp.dma_start(bias[C:C + WIN, 0, :], bias[0:WIN, 0, :]).then_inc(s_tl, 16)
                        sp.wait_ge(s_tl, first + 16)

                with nc.Block() as block:
                    @block.vector
                    def _(dve):
                        split_weights(dve, layer, tw[:, TW["w1"]:TW["w1"] + FF])
                        for kind in (3, 2, 1, 0):
                            o = bias[:, kind, :].rearrange("p (h m) -> p h m", h=HEADS)
                            i = bias[:, 0, :].rearrange("p (h m) -> p h m", h=HEADS)
                            dve.tensor_tensor(o, i, amask[:, kind, :].unsqueeze(1).broadcast_to([P, HEADS, WIN]),
                                              ALU.add).then_inc(s_bt, 1)

            def swin_attention(it, p, base, shift):
                def at(kind, n, k):
                    return it * n + k + 1

                def residuals(s):
                    return p * (NW * NRES) + NRES * (s + 1)

                def strip_x(s):
                    x = xcols(p, base + s * STRIP, STRIP).rearrange("p (row c) -> p row c", row=WS)
                    w = psb[:, :].rearrange("p (win row c) -> p win row c", win=NW, row=WS)
                    if not shift:
                        return [(x.rearrange("p row (win c) -> p win row c", win=NW), w)]
                    m = (NW - 1) * WS
                    return [(x[:, :, shift:shift + m].rearrange("p row (win c) -> p win row c", win=NW - 1), w[:, 0:NW - 1, :, :]),
                            (x[:, :, shift + m:GRID], w[:, NW - 1, :, 0:WS - shift]),
                            (x[:, :, 0:shift], w[:, NW - 1, :, WS - shift:WS])]

                NRES = 3 if shift else 1
                SLOTS = NG + 9

                with nc.Block() as block:
                    @block.tensor
                    def _(pe):
                        for i in range(-3, SLOTS):
                            s, r = divmod(i - NW - 5, NW)
                            if r == 0 and 0 <= s < NW:
                                pe.wait_ge(sa["oev"], at("oev", NW, s))
                                pe.wait_ge(sa["kev"], at("kev", NW, min(s + 1, NW - 1)))
                                if s == NW - 1:
                                    pe.wait_ge(sa["pev"], at("pev", NW, s - 1))
                                pe.matmul(banks[0][:, 0:STRIP], tw[:, TW["p"]:TW["p"] + P], osb,
                                          start=True, stop=True).then_inc(sa["pj"], 1)
                            if 0 <= i < NG:
                                if i % 4 == 0:
                                    if i:
                                        pe.wait_ge(sa["vev"], at("vev", NG // 4, i // 4 - 1))
                                    for n in range(4):
                                        for e in range(2):
                                            last = pe.matmul(banks[5][e * C:(e + 1) * C, n * P:(n + 1) * P],
                                                             XN[:, (i + n) * WIN:(i + n) * WIN + C],
                                                             tw[:, TW["v0"] + e * P:TW["v0"] + (e + 1) * P],
                                                             start=True, stop=True)
                                    last.then_inc(sa["v"], 1)
                                pe.wait_ge(sa["kbd"], at("kbd", NG, i))
                                if i % NW == 0:
                                    pe.wait_ge(sa["qev"], at("qev", NW, i // NW))
                                if i >= 2:
                                    pe.wait_ge(sa["add"], at("add", NG, i - 2))
                                pe.matmul(banks[1 + i % 2][:, 0:HEADS * WIN], qbd[:, (i // NW) % 2, i % NW, :],
                                          kbd[:, i % 4, :, :], start=True, stop=True).then_inc(sa["s"], 1)
                            g = i - 3
                            if 0 <= g < NG:
                                pe.wait_ge(sa["exp"], at("exp", NG, g))
                                if g >= 2:
                                    pe.wait_ge(sa["tev"], at("tev", NG, g - 2))
                                for j in range(4):
                                    last = pe.transpose(banks[3 + g % 2][:, j * P:(j + 1) * P],
                                                        prob[:, g % 3, 2 * j:2 * j + 2, :], ident[:, :])
                                last.then_inc(sa["t"], 1)
                            g = i - 4
                            if 0 <= g < NG:
                                pe.wait_ge(sa["tev"], at("tev", NG, g))
                                pe.wait_ge(sa["vev"], at("vev", NG // 4, g // 4))
                                if g:
                                    pe.wait_ge(sa["nrm"], at("nrm", NG, g - 1))
                                av = banks[6][:, 0:144].rearrange("p (win c) -> p win c", win=2)
                                v = vb[:, g % 8, :, :, :].rearrange("p w h d -> p w (h d)")
                                for j in range(4):
                                    a, b = 2 * j * (HD + 1), (2 * j + 2) * (HD + 1)
                                    last = pe.matmul(av[:, :, a:b], probT[:, g % 2, j, :], v[:, :, a:b],
                                                     start=True, stop=True)
                                last.then_inc(sa["av"], 1)
                            g = i - 5
                            if 0 <= g < NG:
                                pe.wait_ge(sa["nrm"], at("nrm", NG, g))
                                if g % NW == 0 and g:
                                    pe.wait_ge(sa["oev"], at("oev", NW, g // NW - 1))
                                pe.matmul(banks[7][:, (g % NW) * WIN:(g % NW + 1) * WIN], obd[:, g % 2, :],
                                          stack[:, :], start=True, stop=True).then_inc(sa["ot"], 1)
                            s, r = divmod(i + 3, NW)
                            if r == 0 and s < NW:
                                if s >= 2:
                                    pe.wait_ge(sa["pev"], at("pev", NW, s - 2))
                                pe.matmul(banks[0][:, 0:STRIP], tw[:, TW["q"]:TW["q"] + P],
                                          XN[:, s * STRIP:(s + 1) * STRIP], start=True, stop=True).then_inc(sa["q"], 1)
                            if r == 1 and s < NW:
                                pe.wait_ge(sa["qev"], at("qev", NW, s))
                                pe.matmul(banks[0][:, 0:STRIP], tw[:, TW["k"]:TW["k"] + P],
                                          XN[:, s * STRIP:(s + 1) * STRIP], start=True, stop=True).then_inc(sa["k"], 1)

                    @block.scalar
                    def _(act):
                        for i in range(-3, SLOTS):
                            g = i - 1
                            if 0 <= g < NG:
                                act.wait_ge(sa["sub"], at("sub", NG, g))
                                if g >= 3:
                                    act.wait_ge(sa["t"], at("t", NG, g - 3))
                                act.activation(prob[:, g % 3, :, 0:WIN], ssb[:, g % 3, :, :], ACT.Exp)\
                                    .then_inc(sa["exp"], 1)
                            g = i - 3
                            if 0 <= g < NG:
                                act.wait_ge(sa["t"], at("t", NG, g))
                                if g >= 2:
                                    act.wait_ge(sa["av"], at("av", NG, g - 2))
                                act.activation(probT[:, g % 2, :, :].rearrange("p a b -> p (a b)"), banks[3 + g % 2][:, :],
                                               ACT.Copy).then_inc(sa["tev"], 1)
                            s, r = divmod(i - NW - 4, NW)
                            if r == 0 and 0 <= s < NW:
                                act.wait_ge(sa["ot"], at("ot", NG, NW * s + NW - 1))
                                if s:
                                    act.wait_ge(sa["pj"], at("pj", NW, s - 1))
                                act.activation(osb, banks[7][:, 0:STRIP], ACT.Identity,
                                               bias=tv[:, TV["v"]:TV["v"] + 1]).then_inc(sa["oev"], 1)
                            s, r = divmod(i - NW - 5, NW)
                            if r == 0 and 0 <= s < NW:
                                act.wait_ge(sa["pj"], at("pj", NW, s))
                                if s:
                                    act.wait_ge(s_res[shift], residuals(s - 1))
                                act.activation(psb[:, :], banks[0][:, 0:STRIP], ACT.Identity,
                                               bias=tv[:, TV["p"]:TV["p"] + 1]).then_inc(sa["pev"], 1)
                            s, r = divmod(i + 3, NW)
                            if r == 0 and s < NW:
                                act.wait_ge(sa["q"], at("q", NW, s))
                                if s >= 2:
                                    act.wait_ge(sa["s"], at("s", NG, NW * (s - 1) - 1))
                                for h in range(2):
                                    r0, r1 = h * C, (h + 1) * C
                                    last = act.activation(
                                        qbd[r0:r1, s % 2, :, r0:r0 + WIN],
                                        banks[0][r0:r1, 0:STRIP].rearrange("p (win n) -> p win n", win=NW),
                                        ACT.Identity, bias=tv[r0:r1, TV["q"]:TV["q"] + 1])
                                last.then_inc(sa["qev"], 1)
                            if r == 1 and s < NW:
                                act.wait_ge(sa["k"], at("k", NW, s))
                                if s >= 2:
                                    act.wait_ge(sa["kbd"], at("kbd", NG, NW * (s - 1) - 1))
                                act.activation(ksb[:, s % 2, :], banks[0][:, 0:STRIP], ACT.Identity,
                                               bias=tv[:, TV["k"]:TV["k"] + 1]).then_inc(sa["kev"], 1)

                    @block.vector
                    def _(dve):
                        for i in range(SLOTS):
                            if i < NG:
                                dve.wait_ge(sa["s"], at("s", NG, i))
                                if i >= 3:
                                    dve.wait_ge(sa["exp"], at("exp", NG, i - 3))
                                kind = 2 * (i // NW == NW - 1) + (i % NW == NW - 1) if shift else 0
                                sv = ssb[:, i % 3, :, :]
                                dve.scalar_tensor_tensor(sv.rearrange("p h m -> p (h m)"), banks[1 + i % 2][:, 0:HEADS * WIN],
                                                         QSCALE, bias[:, kind, :], ALU.mult, ALU.add)\
                                    .then_inc(sa["add"], 1)
                                if i % 4 == 0:
                                    n = i // 4
                                    dve.wait_ge(sa["v"], at("v", NG // 4, n))
                                    if n >= 2:
                                        dve.wait_ge(sa["av"], at("av", NG, i - 5))
                                    for e in range(2):
                                        r0, r1 = e * C, (e + 1) * C
                                        o = vb[r0:r1, 4 * (n % 2):4 * (n % 2) + 4, :, :, 0:HD]\
                                            .rearrange("p a w (j e) d -> p (a w j) e d", e=2)
                                        v = banks[5][r0:r1, :].rearrange("p (x e d) -> p x e d", e=2, d=HD)
                                        last = dve.tensor_copy(o[:, :, e, :], v[:, :, e, :])
                                    last.then_inc(sa["vev"], 1)
                                dve.wait_ge(sa["add"], at("add", NG, i))
                                dve.tensor_reduce(smax[:, i % 3, :], sv, op=ALU.max, axis=AX.X).then_inc(sa["max"], 1)
                            g = i - 4
                            if 0 <= g < NG:
                                dve.wait_ge(sa["av"], at("av", NG, g))
                                av = banks[6][:, 0:144].rearrange("p (win h d) -> p win h d", win=2, h=HEADS)
                                dve.reciprocal(rcp[:, g % 2, :], av[:, 0, :, HD]).then_inc(sa["rcp"], 1)
                                dve.wait_ge(sa["rcp"], at("rcp", NG, g))
                                if g >= 2:
                                    dve.wait_ge(sa["ot"], at("ot", NG, g - 2))
                                for h in range(2):
                                    r0, r1 = h * C, (h + 1) * C
                                    last = dve.tensor_tensor(
                                        obd[r0:r1, g % 2, r0:r1].rearrange("p (h d) -> p h d", d=HD),
                                        av[r0:r1, h, :, 0:HD],
                                        rcp[r0:r1, g % 2, :].unsqueeze(2).broadcast_to([C, HEADS, HD]), ALU.mult)
                                last.then_inc(sa["nrm"], 1)

                    @block.gpsimd
                    def _(pool):
                        for i in range(-2, SLOTS):
                            g = i + 2
                            if 0 <= g < NG:
                                if g % NW == 0:
                                    pool.wait_ge(sa["kev"], at("kev", NW, g // NW))
                                if g >= 4:
                                    pool.wait_ge(sa["s"], at("s", NG, g - 4))
                                k = ksb[:, (g // NW) % 2, (g % NW) * WIN:(g % NW + 1) * WIN]
                                pool.tensor_tensor(kbd[:, g % 4, :, :], k.unsqueeze(1).broadcast_to([P, HEADS, WIN]),
                                                   headmask[:, :].unsqueeze(2).broadcast_to([P, HEADS, WIN]), ALU.mult)\
                                    .then_inc(sa["kbd"], 1)
                            if 0 <= i < NG:
                                pool.wait_ge(sa["max"], at("max", NG, i))
                                pool.tensor_tensor(ssb[:, i % 3, :, :], ssb[:, i % 3, :, :],
                                                   smax[:, i % 3, :].unsqueeze(2).broadcast_to([P, HEADS, WIN]),
                                                   ALU.subtract).then_inc(sa["sub"], 1)
                            s, r = divmod(i - NW - 5, NW)
                            if r == 0 and 0 <= s < NW:
                                pool.wait_ge(sa["pev"], at("pev", NW, s))
                                for x, w in strip_x(s):
                                    pool.tensor_tensor(x, x, w, ALU.add).then_inc(s_res[shift], 1)

            def rolled(p, shift):
                def pieces(k, o):
                    x = xcols(p, shift * GRID + k * STRIP, STRIP)
                    if not shift:
                        return [(o, x)]
                    x = x.rearrange("p (row c) -> p row c", row=WS)
                    o = o.rearrange("p (row c) -> p row c", row=WS)
                    return [(o[:, :, 0:GRID - shift], x[:, :, shift:GRID]), (o[:, :, GRID - shift:GRID], x[:, :, 0:shift])]
                return pieces

            s_cp = sem("rows_copied")
            for layer, shift in enumerate((0, SHIFT)):
                swin_load(layer)
                base = shift * GRID
                if shift:
                    with nc.Block() as block:
                        @block.vector
                        def _(dve):
                            x = X[:, :].rearrange("p (a n) -> p a n", a=PAIRS)
                            dve.tensor_copy(x[:, :, TOK:TOK + base], x[:, :, 0:base]).then_inc(s_cp, 1)
                with nc.Fori(0, PAIRS) as p:
                    layer_norm(p * 2 + PAIRS * (1 + 2 * layer), STRIP, rolled(p, shift),
                               lambda k: XN[:, k * STRIP:(k + 1) * STRIP]
                               .rearrange("p (win row c) -> p win row c", win=NW, row=WS),
                               windows, (tv[:, TV["g1"]:TV["g1"] + 1], tv[:, TV["b1"]:TV["b1"] + 1]),
                               plain=lambda k: XN[:, k * STRIP:(k + 1) * STRIP])
                    swin_attention(p + layer * PAIRS if layer else p, p, base, shift)
                    layer_norm(p * 2 + PAIRS * (1 + 2 * layer) + 1, STRIP, lambda k, o: [(o, xcols(p, base + k * STRIP, STRIP))],
                               lambda k: XN[:, k * STRIP:(k + 1) * STRIP], flat,
                               (tv[:, TV["g2"]:TV["g2"] + 1], tv[:, TV["b2"]:TV["b2"] + 1]))
                    feed_forward(p + layer * PAIRS, p, STRIP, base,
                                 tw[:, TW["w2"]:TW["w2"] + 2 * C],
                                 tv[:, TV["f1"]:TV["f1"] + 2], tv[:, TV["f2"]:TV["f2"] + 1])

        s_tab = sem("positions_loaded")
        s_sp = sem("h_put_aside")
        s_pos = sem("positions_added")
        with nc.Block() as block:
            @block.sync
            def _(sp):
                sp.dma_start(KS[:, :], t["positions"]).then_inc(s_tab, 16)
                sp.wait_ge(s_tab, 16)
        with nc.Fori(0, PAIRS) as p:
            with nc.Block() as block:
                @block.sync
                def _(sp):
                    sp.dma_start(h_dram[bass.ds(p, 1), :, :].rearrange("a k n -> k (a n)"), xcols(p, BASE, SEQP))\
                        .then_inc(s_sp, 16)
                    sp.wait_ge(s_sp, p * 16 + 16)
                    sp.sem_inc(s_arrived, 1)
            layer_norm(p + 5 * PAIRS, CW, lambda k, o: [(o, xcols(p, BASE + k * CW, CW))],
                       lambda k: xcols(p, BASE + k * CW, CW), flat, None)
            half = SEQP // 2
            with nc.Block() as block:
                @block.vector
                def _(dve):
                    x = xcols(p, BASE, half)
                    dve.tensor_tensor(x, x, KS[:, 0:half], ALU.add).then_inc(s_pos, 1)

                @block.gpsimd
                def _(pool):
                    x = xcols(p, BASE + half, half)
                    pool.tensor_tensor(x, x, KS[:, half:SEQP], ALU.add).then_inc(s_pos, 1)

        with ExitStack() as lin:
            def sbl(name, shape, dt=F32):
                return lin.enter_context(nc.sbuf_tensor(name, shape, dt))

            lw = sbl("lw", [P, LW_N])
            lv = sbl("lv", [P, LV_N])
            kmax = sbl("kmax", [P, CH])
            nkmax = sbl("nkmax", [P, 1])
            ksum = sbl("ksum", [P, CH])
            ksum1 = sbl("ksum1", [P, 1])
            rk = sbl("rk", [P, 1])
            ctm = sbl("ctm", [P, P])
            mix = sbl("mix", [P, P])
            kv = sbl("kv", [TT, 4, 2, 2 * P])
            qs = sbl("qs", [TT, 4, TPC * P])
            qm = sbl("qm", [TT, 2, TPC * 2 * HEADS])
            qd = sbl("qd", [TT, 2, TPC * 2 * HEADS])
            qr = sbl("qr", [TT, 2, TPC * 2 * HEADS])
            qT = sbl("qT", [P, 2, CW])
            s_ll = sem("lin_loaded")
            s_z = sem("lin_cleared")
            sl = {n: sem("lin_" + n) for n in (
                "k", "copy", "max", "nmax", "exp", "sum", "rk", "kv", "kvev", "ctx", "mask", "mix", "mixev",
                "q", "qmax", "qsub", "qexp", "qsum", "qrcp", "qnrm", "qt", "qtev", "out", "res")}
            NQ = NT // 2
            LAYERS = 4

            with nc.Block() as block:
                @block.vector
                def _(dve):
                    dve.memset(KS[:, SEQ:SEQP], 0.0).then_inc(s_z, 1)

            def keys(it):
                def valid(k):
                    return LAST if k == CH - 1 else CW

                with nc.Block() as block:
                    @block.tensor
                    def _(pe):
                        for k in range(CH):
                            if k >= 4:
                                pe.wait_ge(sl["copy"], it * CH + k - 3)
                            pe.matmul(banks[k % 4][:, 0:CW], lw[:, LW["k"]:LW["k"] + P], XN[:, k * CW:(k + 1) * CW],
                                      start=True, stop=True).then_inc(sl["k"], 1)

                    @block.scalar
                    def _(act):
                        for k in range(CH):
                            act.wait_ge(sl["k"], it * CH + k + 1)
                            act.activation(KS[:, k * CW:k * CW + valid(k)], banks[k % 4][:, 0:valid(k)], ACT.Copy)\
                                .then_inc(sl["copy"], 1)
                        act.wait_ge(sl["nmax"], it + 1)
                        act.wait_ge(sl["copy"], it * CH + CH)
                        for k in range(CH):
                            v = KS[:, k * CW:k * CW + valid(k)]
                            act.activation(v, v, ACT.Exp, bias=nkmax[:, :], accum_out=ksum[:, k:k + 1])\
                                .then_inc(sl["exp"], 1)

                    @block.vector
                    def _(dve):
                        for k in range(CH):
                            dve.wait_ge(sl["copy"], it * CH + k + 1)
                            dve.tensor_reduce(kmax[:, k:k + 1], KS[:, k * CW:k * CW + valid(k)], op=ALU.max, axis=AX.X)\
                                .then_inc(sl["max"], 1)
                        dve.wait_ge(sl["max"], it * CH + CH)
                        dve.tensor_reduce(nkmax[:, :], kmax[:, :], op=ALU.max, axis=AX.X, negate=True)\
                            .then_inc(sl["nmax"], 1)
                        dve.wait_ge(sl["exp"], it * CH + CH)
                        dve.tensor_reduce(ksum1[:, :], ksum[:, :], op=ALU.add, axis=AX.X).then_inc(sl["sum"], 1)
                        dve.wait_ge(sl["sum"], it + 1)
                        dve.reciprocal(rk[:, :], ksum1[:, :]).then_inc(sl["rk"], 1)

            def context(it):
                with nc.Block() as block:
                    @block.tensor
                    def _(pe):
                        for i in range(NQ + 2):
                            if i < NQ:
                                if i >= 4:
                                    pe.wait_ge(sl["kvev"], it * NQ + i - 3)
                                b = banks[i % 4]
                                for n in range(2):
                                    a = (2 * i + n) * TT
                                    pe.transpose(b[0:TT, n * 2 * P:n * 2 * P + P], KS[:, a:a + TT], ident[:, :])
                                    last = pe.matmul(b[0:TT, n * 2 * P + P:(n + 1) * 2 * P], XN[:, a:a + TT],
                                                     lw[:, LW["v"]:LW["v"] + P], start=True, stop=True)
                                last.then_inc(sl["kv"], 1)
                            g = i - 2
                            if g >= 0:
                                pe.wait_ge(sl["kvev"], it * NQ + g + 1)
                                for n in range(2):
                                    last = pe.matmul(banks[7][:, 0:P], kv[:, g % 4, n, P:2 * P], kv[:, g % 4, n, 0:P],
                                                     start=(g == 0 and n == 0), stop=(g == NQ - 1 and n == 1))
                                last.then_inc(sl["ctx"], 1)
                        pe.wait_ge(sl["mask"], it + 1)
                        pe.matmul(banks[6][:, 0:P], ctm[:, :], lw[:, LW["o"]:LW["o"] + P], start=True, stop=True)\
                            .then_inc(sl["mix"], 1)

                    def evacuate(i):
                        return kv[:, i % 4, :, :].rearrange("p a b -> p (a b)"), banks[i % 4][0:TT, :]

                    @block.scalar
                    def _(act):
                        for i in range(0, NQ, 2):
                            act.wait_ge(sl["kv"], it * NQ + i + 1)
                            if i >= 4:
                                act.wait_ge(sl["ctx"], it * NQ + i - 3)
                            if i:
                                act.wait_ge(sl["kvev"], it * NQ + i)
                            o, b = evacuate(i)
                            act.activation(o, b, ACT.Copy).then_inc(sl["kvev"], 1)

                    @block.vector
                    def _(dve):
                        for i in range(1, NQ, 2):
                            dve.wait_ge(sl["kv"], it * NQ + i + 1)
                            if i >= 4:
                                dve.wait_ge(sl["ctx"], it * NQ + i - 3)
                            dve.wait_ge(sl["kvev"], it * NQ + i)
                            o, b = evacuate(i)
                            dve.tensor_copy(o, b).then_inc(sl["kvev"], 1)
                        dve.wait_ge(sl["ctx"], it * NQ + NQ)
                        dve.tensor_tensor(ctm[:, :], banks[7][:, 0:P], bdmask[:, :], ALU.mult).then_inc(sl["mask"], 1)
                        dve.wait_ge(sl["mix"], it + 1)
                        dve.tensor_scalar(mix[:, :], banks[6][:, 0:P], rk[:, :], QSCALE, ALU.mult, ALU.mult)\
                            .then_inc(sl["mixev"], 1)

            def queries(it, p):
                def done(k):
                    return it * CH + k + 1

                G = TPC * 2 * HEADS
                with nc.Block() as block:
                    @block.tensor
                    def _(pe):
                        for i in range(CH + 3):
                            if i < CH:
                                if i >= 2:
                                    pe.wait_ge(sl["qsub"], done(i - 2))
                                for n in range(TPC):
                                    a = i * CW + n * TT
                                    last = pe.matmul(banks[i % 2][0:TT, n * P:(n + 1) * P], XN[:, a:a + TT],
                                                     lw[:, LW["q"]:LW["q"] + P], start=True, stop=True)
                                last.then_inc(sl["q"], 1)
                            k = i - 2
                            if 0 <= k < CH:
                                pe.wait_ge(sl["qnrm"], done(k))
                                if k >= 2:
                                    pe.wait_ge(sl["qtev"], done(k - 2))
                                for n in range(TPC):
                                    last = pe.transpose(banks[2 + k % 2][:, n * TT:(n + 1) * TT],
                                                        qs[:, k % 4, n * P:(n + 1) * P], ident[0:TT, 0:TT])
                                last.then_inc(sl["qt"], 1)
                            k = i - 3
                            if k >= 0:
                                pe.wait_ge(sl["qtev"], done(k))
                                if k >= 2:
                                    pe.wait_ge(sl["res"], done(k - 2))
                                pe.matmul(banks[4 + k % 2][:, 0:CW], mix[:, :], qT[:, k % 2, :],
                                          start=True, stop=True).then_inc(sl["out"], 1)

                    @block.vector
                    def _(dve):
                        for i in range(CH + 3):
                            if i < CH:
                                dve.wait_ge(sl["q"], done(i))
                                if i >= 4:
                                    dve.wait_ge(sl["qt"], done(i - 4))
                                b = banks[i % 2][0:TT, :].rearrange("p (g d) -> p g d", d=HD)
                                q = qs[:, i % 4, :].rearrange("p (g d) -> p g d", d=HD)
                                dve.tensor_reduce(qm[:, i % 2, :], b, op=ALU.max, axis=AX.X).then_inc(sl["qmax"], 1)
                                dve.wait_ge(sl["qmax"], done(i))
                                dve.tensor_tensor(q, b, qm[:, i % 2, :].unsqueeze(2).broadcast_to([TT, G, HD]),
                                                  ALU.subtract).then_inc(sl["qsub"], 1)
                            k = i - 1
                            if 0 <= k < CH:
                                dve.wait_ge(sl["qexp"], done(k))
                                q = qs[:, k % 4, :].rearrange("p (g d) -> p g d", d=HD)
                                dve.tensor_reduce(qd[:, k % 2, :], q, op=ALU.add, axis=AX.X).then_inc(sl["qsum"], 1)
                                if k >= 2:
                                    dve.wait_ge(sl["qnrm"], done(k - 2))
                                dve.wait_ge(sl["qsum"], done(k))
                                dve.reciprocal(qr[:, k % 2, :], qd[:, k % 2, :]).then_inc(sl["qrcp"], 1)
                            k = i - 3
                            if k >= 0:
                                dve.wait_ge(sl["out"], done(k))
                                x = xcols(p, BASE + k * CW, CW)
                                dve.scalar_tensor_tensor(x, banks[4 + k % 2][:, 0:CW], lv[:, LV["o"]:LV["o"] + 1], x,
                                                         ALU.add, ALU.add).then_inc(sl["res"], 1)

                    @block.scalar
                    def _(act):
                        for i in range(CH + 2):
                            if i < CH:
                                act.wait_ge(sl["qsub"], done(i))
                                act.activation(qs[:, i % 4, :], qs[:, i % 4, :], ACT.Exp).then_inc(sl["qexp"], 1)
                            k = i - 2
                            if k >= 0:
                                act.wait_ge(sl["qt"], done(k))
                                if k >= 2:
                                    act.wait_ge(sl["out"], done(k - 2))
                                act.activation(qT[:, k % 2, :], banks[2 + k % 2][:, 0:CW], ACT.Copy)\
                                    .then_inc(sl["qtev"], 1)

                    @block.gpsimd
                    def _(pool):
                        for k in range(CH):
                            pool.wait_ge(sl["qrcp"], done(k))
                            q = qs[:, k % 4, :].rearrange("p (g d) -> p g d", d=HD)
                            pool.tensor_tensor(q, q, qr[:, k % 2, :].unsqueeze(2).broadcast_to([TT, G, HD]), ALU.mult)\
                                .then_inc(sl["qnrm"], 1)

            with nc.Fori(0, LAYERS) as l:
                with nc.Block() as block:
                    @block.sync
                    def _(sp):
                        sp.dma_start(lw[:, :], t["lin_w"][bass.ds(l, 1), :, :].rearrange("a k n -> k (a n)"))\
                            .then_inc(s_ll, 16)
                        sp.dma_start(lv[:, :], t["lin_v"][bass.ds(l, 1), :, :].rearrange("a k n -> k (a n)"))\
                            .then_inc(s_ll, 16)
                        sp.wait_ge(s_ll, l * 32 + 32)
                        sp.sem_inc(s_arrived, 1)

                    @block.vector
                    def _(dve):
                        dve.wait_ge(s_ll, l * 32 + 32)
                        split_weights(dve, l + 2, lw[:, LW["w1"]:LW["w1"] + FF])
                with nc.Fori(0, PAIRS) as p:
                    it = l * PAIRS + p
                    stream = lambda k, o: [(o, xcols(p, BASE + k * CW, CW))]
                    normal = lambda k: XN[:, k * CW:(k + 1) * CW]
                    layer_norm(it * 2 + 6 * PAIRS, CW, stream, normal, flat,
                               (lv[:, LV["g1"]:LV["g1"] + 1], lv[:, LV["b1"]:LV["b1"] + 1]))
                    keys(it)
                    context(it)
                    queries(it, p)
                    layer_norm(it * 2 + 6 * PAIRS + 1, CW, stream, normal, flat,
                               (lv[:, LV["g2"]:LV["g2"] + 1], lv[:, LV["b2"]:LV["b2"] + 1]))
                    feed_forward(it + 2 * PAIRS, p, CW, BASE,
                                 lw[:, LW["w2"]:LW["w2"] + 2 * C],
                                 lv[:, LV["f1"]:LV["f1"] + 2], lv[:, LV["f2"]:LV["f2"] + 1])

        with ExitStack() as moe:
            def sbm(name, shape, dt=F32):
                return moe.enter_context(nc.sbuf_tensor(name, shape, dt))

            U = 2 * EXP
            W3 = 3 * U
            mw = sbm("mw", [P, MW_N])
            mv = sbm("mv", [P, MV_N])
            w1e = sbm("w1e", [P, 2, EXP * P], F32R)
            br = sbm("br", [TT, U])
            rank = sbm("rank", [TT, U])
            b2f = sbm("b2f", [W3, P])
            b2p = sbm("b2p", [W3, 3, P], BF16)
            sel = sbm("sel", [W3, U, P], BF16)
            lg = sbm("lg", [TT, NT, U])
            r1 = sbm("r1", [TT, NT, U])
            r2 = sbm("r2", [TT, NT, U])
            o1 = sbm("o1", [TT, NT, U])
            o2 = sbm("o2", [TT, NT, U])
            ws3 = sbm("ws3", [TT, NT + 2, 3, U], BF16)
            m1 = sbm("m1", [TT, NT * 2])
            m2 = sbm("m2", [TT, NT * 2])
            mr = sbm("mr", [TT, NT * 2])
            ed = sbm("ed", [TT, NT * 2])
            w1s = sbm("w1s", [TT, NT * 2])
            w2s = sbm("w2s", [TT, NT * 2])
            wT = sbm("wT", [W3, SEQP], BF16)
            identb = sbm("identb", [TT, TT], BF16)
            yb = sbm("yb", [P, 2, CW])
            ob = sbm("ob", [TT, 2, TPC * P])
            w1f = XN[:, 0:EXP * P]
            self32 = hid[0:W3, :, :].rearrange("p a n -> p (a n)")[:, 0:U * P].rearrange("p (u n) -> p u n", u=U)
            s_ml = sem("moe_loaded")
            s_b2 = sem("moe_b2_parts")
            s_wc = sem("moe_cleared")
            s_rh = sem("moe_h_back")
            s_ha = sem("moe_h_added")
            sm = {n: sem("moe_" + n) for n in (
                "logits", "step", "diff", "edge", "wt", "wtev", "up", "gelu", "bc", "gated", "down", "y", "yt", "yev",
                "out0", "out1")}

            with nc.Block() as block:
                @block.sync
                def _(sp):
                    for dst, name in ((mw[:, :], "moe_w"), (mv[:, :], "moe_v"), (br[:, :], "moe_br"),
                                      (rank[:, :], "rank"), (b2f[:, :], "moe_b2"), (self32, "sel"), (w1f, "moe_w1")):
                        sp.dma_start(dst, t[name]).then_inc(s_ml, 16)
                    sp.wait_ge(s_ml, 7 * 16)

                @block.vector
                def _(dve):
                    dve.wait_ge(s_ml, 7 * 16)
                    dve.tensor_copy(w1e[:, 0, :], w1f).then_inc(s_w1h, 1)
                    dve.wait_ge(s_w1h, 7)
                    dve.tensor_tensor(w1e[:, 1, :], w1f, w1e[:, 0, :].bitcast(F32), ALU.subtract).then_inc(s_w1l, 1)
                    dve.tensor_copy(sel[:, :, :], self32).then_inc(s_wc, 1)
                    dve.tensor_copy(identb[:, :], ident[0:TT, 0:TT]).then_inc(s_wc, 1)
                    dve.memset(ws3[:, NT:NT + 2, :, :], 0.0).then_inc(s_wc, 1)
                    for n in range(3):
                        dve.tensor_copy(b2p[:, n, :], b2f[:, :]).then_inc(s_b2, 1)
                        if n < 2:
                            dve.wait_ge(s_b2, 2 * n + 1)
                            dve.tensor_tensor(b2f[:, :], b2f[:, :], b2p[:, n, :], ALU.subtract).then_inc(s_b2, 1)
                            dve.wait_ge(s_b2, 2 * n + 2)

            def route(it):
                STEPS = 23

                with nc.Block() as block:
                    @block.tensor
                    def _(pe):
                        for n in range(NT):
                            last = pe.matmul(banks[0][0:TT, n * U:(n + 1) * U], XN[:, n * TT:(n + 1) * TT],
                                             mw[:, MW["r"]:MW["r"] + U], start=True, stop=True)
                        last.then_inc(sm["logits"], 1)
                        pe.wait_ge(sm["step"], it * STEPS + STEPS)
                        for k in range(CH):
                            if k >= 2:
                                pe.wait_ge(sm["wtev"], it * CH + k - 1)
                            b = banks[1 + k % 2][:, :].bitcast(BF16)
                            parts = ws3[:, :, :, :].rearrange("p t a u -> p (t a u)")
                            for n in range(TPC):
                                a = (k * TPC + n) * W3
                                last = pe.transpose(b[:, n * P:n * P + TT], parts[:, a:a + P], identb[:, :])
                            last.then_inc(sm["wt"], 1)

                    @block.scalar
                    def _(act):
                        act.wait_ge(sm["diff"], it + 1)
                        act.activation(ed[:, :], ed[:, :], ACT.Exp).then_inc(sm["edge"], 1)
                        for k in range(CH):
                            act.wait_ge(sm["wt"], it * CH + k + 1)
                            b = banks[1 + k % 2][0:W3, :].bitcast(BF16).rearrange("p (n c) -> p n c", c=P)
                            act.activation(wT[:, k * CW:(k + 1) * CW].rearrange("p (n c) -> p n c", c=TT),
                                           b[:, 0:TPC, 0:TT], ACT.Copy).then_inc(sm["wtev"], 1)

                    @block.vector
                    def _(dve):
                        count = [0]

                        def then(ins):
                            count[0] += 1
                            ins.then_inc(sm["step"], 1)
                            if count[0] < STEPS:
                                dve.wait_ge(sm["step"], it * STEPS + count[0])

                        def grouped(v):
                            return v[:, :, :].rearrange("p t (h e) -> p (t h) e", h=2)

                        def each(v):
                            return v[:, :].unsqueeze(2).broadcast_to([TT, NT * 2, EXP])

                        def tiles(v):
                            return v[:, :].unsqueeze(1).broadcast_to([TT, NT, U])

                        def first_of(one, best):
                            then(dve.tensor_tensor(grouped(r1), grouped(lg), each(best), ALU.is_equal))
                            then(dve.tensor_tensor(r1[:, :, :], r1[:, :, :], tiles(rank), ALU.mult))
                            then(dve.tensor_reduce(mr[:, :], grouped(r1), op=ALU.max, axis=AX.X))
                            then(dve.tensor_tensor(grouped(one), grouped(r1), each(mr), ALU.is_equal))

                        dve.wait_ge(sm["logits"], it + 1)
                        then(dve.tensor_tensor(lg[:, :, :], banks[0][0:TT, :].rearrange("p (t u) -> p t u", u=U),
                                               tiles(br), ALU.add))
                        then(dve.tensor_reduce(m1[:, :], grouped(lg), op=ALU.max, axis=AX.X))
                        first_of(o1, m1)
                        then(dve.scalar_tensor_tensor(lg[:, :, :].rearrange("p t u -> p (t u)"),
                                                      o1[:, :, :].rearrange("p t u -> p (t u)"), TOPK_BIG,
                                                      lg[:, :, :].rearrange("p t u -> p (t u)"), ALU.mult, ALU.add))
                        then(dve.tensor_reduce(m2[:, :], grouped(lg), op=ALU.max, axis=AX.X))
                        first_of(o2, m2)
                        dve.tensor_tensor(ed[:, :], m2[:, :], m1[:, :], ALU.subtract).then_inc(sm["diff"], 1)
                        dve.wait_ge(sm["edge"], it + 1)
                        then(dve.tensor_scalar(w1s[:, :], ed[:, :], 1.0, None, ALU.add))
                        then(dve.reciprocal(w1s[:, :], w1s[:, :]))
                        then(dve.tensor_tensor(w2s[:, :], ed[:, :], w1s[:, :], ALU.mult))
                        then(dve.tensor_tensor(grouped(o1), grouped(o1), each(w1s), ALU.mult))
                        then(dve.tensor_tensor(grouped(o2), grouped(o2), each(w2s), ALU.mult))
                        then(dve.tensor_tensor(r2[:, :, :], o1[:, :, :], o2[:, :, :], ALU.add))
                        for n in range(3):
                            then(dve.tensor_copy(ws3[:, 0:NT, n, :], r2[:, :, :]))
                            if n < 2:
                                then(dve.tensor_tensor(r2[:, :, :], r2[:, :, :], ws3[:, 0:NT, n, :], ALU.subtract))
                        assert count[0] == STEPS, count[0]

            def out_pieces(k):
                if k < CH - 1:
                    return [(0, TPC, 0, TT, 1 + BASE + k * CW)]
                found, wrap = [], TOK - BASE
                for n in range(TPC):
                    f = k * CW + n * TT
                    for a, b, to in ((f, min(f + TT, wrap), 1 + BASE + f),
                                     (max(f, wrap), min(f + TT, TOK), 1 + max(f, wrap) - wrap),
                                     (max(f, TOK), min(f + TT, SEQ), 0)):
                        if a < b:
                            found.append((n, 1, a - f, b - a, to))
                return found

            def stores(k):
                return sum(2 * len(out_pieces(c)) for c in range(k % 2, k + 1, 2))

            def experts(it, p):
                def done(n, k):
                    return it * (CH * n) + k + 1

                def outs(k):
                    return it * (16 * stores(CH - 2 + k % 2)) + 16 * stores(k)

                LAG = 4
                with nc.Block() as block:
                    @block.tensor
                    def _(pe):
                        for i in range(CH * U + LAG + 2):
                            if i < CH * U:
                                k, u = divmod(i, U)
                                e, h = divmod(u, 2)
                                c = h * EXP + e
                                if u == 0:
                                    pe.wait_ge(s_lo, (it + 6 * PAIRS) * CH + k + 1)
                                if i >= 2:
                                    pe.wait_ge(sm["gelu"], done(U, i - 2))
                                exact(pe, banks[i % 2][:, 0:CW], w1e[:, 0, e * P:(e + 1) * P],
                                      w1e[:, 1, e * P:(e + 1) * P], xs[:, k % 2, h, :]).then_inc(sm["up"], 1)
                                if i >= 2:
                                    pe.wait_ge(sm["gated"], done(U, i - 2))
                                pe.matmul(banks[2 + i % 2][:, 0:CW], sel[:, c, :], wT[:, k * CW:(k + 1) * CW],
                                          start=True, stop=True).then_inc(sm["bc"], 1)
                            g = i - LAG
                            if 0 <= g < CH * U and g % 2 == 1:
                                k, u = divmod(g, U)
                                e = u // 2
                                d = banks[4 + k % 2]
                                if e == 0:
                                    if k >= 2:
                                        pe.wait_ge(sm["y"], done(1, k - 2))
                                    for n in range(3):
                                        pe.matmul(d[:, 0:CW], b2p[:, n, :], wT[:, k * CW:(k + 1) * CW],
                                                  start=(n == 0), stop=False)
                                pe.wait_ge(sm["gated"], done(U, g))
                                for h in range(2):
                                    last = pe.matmul(d[h * C:(h + 1) * C, 0:CW],
                                                     mw[:, MW["w2"] + e * C:MW["w2"] + (e + 1) * C],
                                                     hid[:, (g - 1 + h) % 8, :], start=False, stop=(e == EXP - 1))
                                last.then_inc(sm["down"], 1)
                            g = i - LAG - 1
                            if g >= 0 and g % U == U - 1 and g // U < CH:
                                k = g // U
                                pe.wait_ge(sm["y"], done(1, k))
                                if k >= 2:
                                    pe.wait_ge(sm["yev"], done(1, k - 2))
                                for n in range(TPC):
                                    last = pe.transpose(banks[6 + k % 2][0:TT, n * P:(n + 1) * P],
                                                        yb[:, k % 2, n * TT:(n + 1) * TT], ident[:, :])
                                last.then_inc(sm["yt"], 1)

                    @block.scalar
                    def _(act):
                        for i in range(CH * U + U):
                            if i < CH * U:
                                e = (i % U) // 2
                                act.wait_ge(sm["up"], done(U, i))
                                if i >= 8:
                                    act.wait_ge(sm["down"], done(EXP, (i - 8) // 2))
                                act.activation(hid[:, i % 8, :], banks[i % 2][:, 0:CW], ACT.Gelu,
                                               bias=mv[:, MV["f1"] + e:MV["f1"] + e + 1]).then_inc(sm["gelu"], 1)
                            g = i - U
                            if g >= 0 and g % U == U - 1:
                                k = g // U
                                act.wait_ge(sm["yt"], done(1, k))
                                if k >= 2:
                                    act.wait_ge(sm[f"out{k % 2}"], outs(k - 2))
                                act.activation(ob[:, k % 2, :], banks[6 + k % 2][0:TT, :], ACT.Copy)\
                                    .then_inc(sm["yev"], 1)

                    @block.vector
                    def _(dve):
                        def used(k):
                            if k >= 2:
                                dve.wait_ge(sm["up"], done(U, U * (k - 1) - 1))

                        split_chunk(dve, it + 6 * PAIRS, 0, CW, lambda: None)
                        for i in range(CH * U + LAG + 1):
                            if i < CH * U:
                                if i % U == 4 and i // U + 1 < CH:
                                    split_chunk(dve, it + 6 * PAIRS, i // U + 1, CW, lambda: used(i // U + 1))
                                dve.wait_ge(sm["gelu"], done(U, i))
                                dve.wait_ge(sm["bc"], done(U, i))
                                v = hid[:, i % 8, :]
                                dve.tensor_tensor(v, v, banks[2 + i % 2][:, 0:CW], ALU.mult).then_inc(sm["gated"], 1)
                            g = i - LAG
                            if g >= 0 and g % U == U - 1:
                                k = g // U
                                dve.wait_ge(sm["down"], done(EXP, k * EXP + EXP - 1))
                                if k >= 2:
                                    dve.wait_ge(sm["yt"], done(1, k - 2))
                                dve.tensor_tensor(yb[:, k % 2, :], banks[4 + k % 2][:, 0:CW],
                                                  xcols(p, BASE + k * CW, CW), ALU.add).then_inc(sm["y"], 1)

                    @block.sync
                    def _(sp):
                        for k in range(CH):
                            sp.wait_ge(sm["yev"], done(1, k))
                            for h in range(2):
                                v = ob[:, k % 2, :].rearrange("p (n h c) -> p n h c", n=TPC, h=2)
                                o = out[bass.ds(p + h * PAIRS if h else p, 1), :, :].rearrange("a n c -> (a n) c")
                                for n0, nn, q0, nq, to in out_pieces(k):
                                    dst = o[to:to + nn * nq, :].rearrange("(n q) c -> q n c", n=nn)
                                    sp.dma_start(dst, v[q0:q0 + nq, n0:n0 + nn, h, :]).then_inc(sm[f"out{k % 2}"], 16)
                        sp.wait_ge(sm["out0"], outs(CH - 2))
                        sp.wait_ge(sm["out1"], outs(CH - 1))
                        sp.sem_inc(s_arrived, 1)

            with nc.Fori(0, PAIRS) as p:
                with nc.Block() as block:
                    @block.sync
                    def _(sp):
                        sp.dma_start(KS[:, :], h_dram[bass.ds(p, 1), :, :].rearrange("a k n -> k (a n)"))\
                            .then_inc(s_rh, 16)
                        sp.wait_ge(s_rh, p * 16 + 16)
                        sp.sem_inc(s_arrived, 1)

                    @block.vector
                    def _(dve):
                        dve.wait_ge(s_rh, p * 16 + 16)
                        x = xcols(p, BASE, SEQP)
                        dve.tensor_tensor(x, x, KS[:, :], ALU.add).then_inc(s_ha, 1)
                normal = lambda k: XN[:, k * CW:(k + 1) * CW]
                layer_norm(p * 2 + 14 * PAIRS, CW, lambda k, o: [(o, xcols(p, BASE + k * CW, CW))], normal, flat, None)
                layer_norm(p * 2 + 14 * PAIRS + 1, CW, lambda k, o: [(o, normal(k))], normal, flat,
                           (mv[:, MV["g"]:MV["g"] + 1], mv[:, MV["b"]:MV["b"] + 1]))
                route(p)
                experts(p, p)


def twice(a):
    return np.concatenate([a, a], axis=0)


def diagonal(a):
    o = np.zeros((2 * a.shape[0], 2 * a.shape[1]), a.dtype)
    o[:a.shape[0], :a.shape[1]] = a
    o[a.shape[0]:, a.shape[1]:] = a
    return o


def second(a):
    return np.concatenate([a[:P], a[P:]], axis=1)


def constants():
    c = {}
    one = np.ones((C, C), np.float32) / C
    c["mean"] = diagonal(one)
    c["centre"] = np.eye(P, dtype=np.float32) - c["mean"]
    c["ident"] = np.eye(P, dtype=np.float32)
    c["bdmask"] = np.kron(np.eye(P // HD, dtype=np.float32), np.ones((HD, HD), np.float32))
    c["headmask"] = twice(np.kron(np.eye(HEADS, dtype=np.float32), np.ones((HD, 1), np.float32)))
    stack = np.zeros((C, WIN), np.float32)
    stack[:WIN] = np.eye(WIN, dtype=np.float32)
    c["stack"] = twice(stack)
    region = np.zeros((2, WS), np.int32)
    region[1, WS - SHIFT:] = 1
    amask = np.zeros((2, P, 4, WIN), np.float32)
    for kind in range(4):
        lab = (region[kind // 2][:, None] * 2 + region[kind % 2][None, :]).reshape(-1)
        m = np.where(lab[:, None] != lab[None, :], -100.0, 0.0).astype(np.float32)
        for h in (0, C):
            amask[1, h:h + WIN, kind, :] = m
    c["amask"] = amask
    pos = np.arange(SEQ, dtype=np.float32)[:, None]
    div = np.exp(np.arange(0, C, 2, dtype=np.float32) * (-np.log(np.float32(10000.0)) / np.float32(C)))
    pe = np.zeros((SEQ, C), np.float32)
    pe[:, 0::2] = np.sin(pos * div)
    pe[:, 1::2] = np.cos(pos * div)
    f = np.arange(SEQ)
    row = np.where(f < TOK - BASE, 1 + BASE + f, 1 + f - (TOK - BASE))
    row[TOK] = 0
    table = np.zeros((C, SEQP), np.float32)
    table[:, :SEQ] = pe[row].T
    c["positions"] = twice(table)
    U = 2 * EXP
    c["rank"] = np.tile(np.arange(EXP, 0, -1, dtype=np.float32), (TT, 2))
    sel = np.zeros((3 * U, U, P), np.float32)
    for part in range(3):
        for u in range(U):
            sel[part * U + u, u, :] = 1.0
    c["sel"] = sel
    return c


def laid_out(i):
    a = {k: np.asarray(v) for k, v in i.items()}
    t = {}
    x = a["x"].reshape(2, PAIRS, GRID, PATCH, GRID, PATCH)
    t["patches"] = np.ascontiguousarray(x.transpose(1, 0, 3, 5, 2, 4)).reshape(PAIRS, 32, TOK)
    t["cls"] = twice(a["cls_tok"].reshape(C, 1))
    g = lambda n: a["L0_tok_" + n]
    t["pe_w"] = diagonal(g("pe_w").reshape(C, PATCH * PATCH).T)
    t["pe_v"] = twice(np.stack([g("pe_b"), g("pe_ng"), g("pe_nb")], axis=1))
    w, v = [], []
    for l in range(2):
        qkv = g("qkv_w")[l].T
        wv = qkv[:, 2 * C:].reshape(C, HEADS // 2, 2, HD)
        masked = []
        for e in range(2):
            m = np.zeros_like(wv)
            m[:, :, e, :] = wv[:, :, e, :]
            masked.append(diagonal(m.reshape(C, C)))
        w.append(np.concatenate([diagonal(qkv[:, :C]), diagonal(qkv[:, C:2 * C]), *masked,
                                 diagonal(g("proj_w")[l].T), twice(g("w1")[l].T), second(g("w2")[l].T)], axis=1))
        b = g("qkv_b")[l]
        f1 = g("b1")[l]
        cols = [g("n1g")[l], g("n1b")[l], b[:C], b[C:2 * C], b[2 * C:], g("proj_b")[l], g("n2g")[l], g("n2b")[l]]
        v.append(np.concatenate([twice(np.stack(cols, axis=1)), f1.reshape(2, P).T,
                                 twice(g("b2")[l][:, None])], axis=1))
    t["tok_w"], t["tok_v"] = np.stack(w), np.stack(v)
    n = 2 * WS - 1
    t["rpb_rev"] = np.ascontiguousarray(g("rpb")[:, ::-1, :].transpose(0, 2, 1)).reshape(2, HEADS, n, n)
    g = lambda n: a["L0_attn_" + n]
    w, v = [], []
    for l in range(4):
        w.append(np.concatenate([diagonal(g("Wk")[l]), diagonal(g("Wq")[l]), diagonal(g("Wv")[l]),
                                 diagonal(g("Wo")[l]), twice(g("W1")[l]), second(g("W2")[l])], axis=1))
        cols = [g("g1")[l], g("b1")[l], g("bo")[l], g("g2")[l], g("b2")[l]]
        v.append(np.concatenate([twice(np.stack(cols, axis=1)), g("bf1")[l].reshape(2, P).T,
                                 twice(g("bf2")[l][:, None])], axis=1))
    t["lin_w"], t["lin_v"] = np.stack(w), np.stack(v)
    g = lambda n: a["L0_ffn_" + n]
    up = g("W1").transpose(1, 0, 2).reshape(C, EXP * P)
    down = g("W2").transpose(1, 0, 2).reshape(P, EXP * C)
    t["moe_w"] = np.concatenate([diagonal(g("Wr")), down], axis=1)
    t["moe_w1"] = twice(up)
    t["moe_v"] = np.concatenate([twice(np.stack([g("gamma"), g("beta")], axis=1)), g("b1").T], axis=1)
    t["moe_br"] = np.tile(g("br"), (TT, 2))
    t["moe_b2"] = np.tile(diagonal(g("b2")), (3, 1))
    return t


def kernel(**inputs):
    import concourse.bacc as _bacc
    from concourse.bass_utils import run_bass_kernel_spmd as _run

    nc = _bacc.Bacc("TRN2", target_bir_lowering=False, num_devices=1)
    arrays, args = {}, {}
    for name, a in {**constants(), **laid_out(inputs)}.items():
        a = np.ascontiguousarray(a)
        arrays[f"in_{name}"] = a
        args[name] = nc.dram_tensor(f"in_{name}", a.shape, mybir.dt.from_np(a.dtype), kind="ExternalInput").ap()
    out = nc.dram_tensor("out_0", (B, SEQ, C), F32, kind="ExternalOutput").ap()
    vit_tower(nc, args, out)
    return _run(nc, [arrays], core_ids=[0]).results[0]["out_0"]
```

```python
from contextlib import ExitStack

import numpy as np

import concourse.bass as bass
from concourse import mybir

F32 = mybir.dt.float32
BF16 = mybir.dt.bfloat16
F32R = mybir.dt.float32r
ALU = mybir.AluOpType
ACT = mybir.ActivationFunctionType
AX = mybir.AxisListType

B, IMG, PATCH = 16, 224, 4
GRID = IMG // PATCH
TOK = GRID * GRID
C, HEADS, HD = 64, 8, 8
PAIRS = B // 2
P = 128
WS, SHIFT = 7, 3
WIN = WS * WS
NW = GRID // WS
STRIP = WS * GRID
SEQ = TOK + 1
CH = 8
TT = 99
TPC = 4
CW = TT * TPC
SEQP = CH * CW
NT = CH * TPC
BASE = SHIFT * GRID
PSTR = BASE + SEQP
FF = 4 * C
EXP, TOPK_BIG = 8, -1.0e38
EPS = 1e-5
QSCALE = float(HD) ** -0.5
LAST = SEQ - (CH - 1) * CW

TW = {"q": 0, "k": 128, "v": 256, "p": 384, "w1": 512, "w2": 512 + FF}
TW_N = TW["w2"] + 2 * C
TV = {"g1": 0, "b1": 1, "q": 2, "k": 3, "v": 4, "p": 5, "g2": 6, "b2": 7, "f1": 8, "f2": 10}
TV_N = 11
LW = {"k": 0, "q": 128, "v": 256, "o": 384, "w1": 512, "w2": 512 + FF}
LW_N = LW["w2"] + 2 * C
LV = {"g1": 0, "b1": 1, "o": 2, "g2": 3, "b2": 4, "f1": 5, "f2": 7}
LV_N = 8
MW = {"r": 0, "w2": 2 * EXP}
MW_N = MW["w2"] + EXP * C
MV = {"g": 0, "b": 1, "f1": 2}
MV_N = 2 + EXP


def vit_tower(nc, t, out):
    ctx = ExitStack()
    with ctx:
        def sb(name, shape, dt=F32):
            return ctx.enter_context(nc.sbuf_tensor(name, shape, dt))

        def sem(name):
            return ctx.enter_context(nc.semaphore(name))

        X = sb("X", [P, PAIRS * PSTR])
        XN = sb("XN", [P, SEQP + 32])
        KS = sb("KS", [P, SEQP])
        sq = sb("sq", [P, 2, CW])
        rs = sb("rs", [P, 2, CW])
        hid = sb("hid", [P, 8, CW])
        xs = sb("xs", [P, 2, 2, CW], F32R)
        w1p = sb("w1p", [P, 2, FF], F32R)
        eps = sb("eps", [P, 1])
        junk = sb("junk", [P, 1])
        centre = sb("centre", [P, P])
        mean = sb("mean", [P, P])
        ident = sb("ident", [P, P])
        bdmask = sb("bdmask", [P, P])
        banks = [ctx.enter_context(nc.psum_tensor(f"bank{i}", [P, 512], F32)) for i in range(8)]

        h_dram = nc.dram_tensor("h_spill", (PAIRS + 1, P, SEQP), F32).ap()

        def xcols(p, a, n):
            return X[:, bass.ds(p * PSTR + a, n)]

        s_load = sem("s_load")
        s_const = sem("s_const")
        s_arrived = sem("dma_arrived")
        s_passed = sem("wait_passed")
        LOADED = 16 * (4 + PAIRS)
        with nc.Block() as block:
            @block.sync
            def _(sp):
                sp.dma_start(centre[:, :], t["centre"]).then_inc(s_load, 16)
                sp.dma_start(mean[:, :], t["mean"]).then_inc(s_load, 16)
                sp.dma_start(ident[:, :], t["ident"]).then_inc(s_load, 16)
                sp.dma_start(bdmask[:, :], t["bdmask"]).then_inc(s_load, 16)
                sp.wait_ge(s_const, 4)
                for p in range(PAIRS):
                    sp.dma_start(X[:, p * PSTR + BASE + TOK:p * PSTR + BASE + TOK + 1], t["cls"],
                                 ).then_inc(s_load, 16)
                sp.wait_ge(s_load, LOADED)

            @block.vector
            def _(dve):
                dve.memset(eps[:, :], EPS).then_inc(s_const, 1)
                dve.memset(XN[:, :], 0.0).then_inc(s_const, 1)
                dve.memset(junk[:, :], 1.0).then_inc(s_const, 1)
                dve.memset(X[:, :].rearrange("p (a n) -> p a n", a=PAIRS)[:, :, BASE + TOK:], 0.0)\
                    .then_inc(s_const, 1)

        s_xc = sem("ln_centred")
        s_sq = sem("ln_squared")
        s_var = sem("ln_variance")
        s_rs = sem("ln_rstd")
        s_xn = sem("ln_normalised")
        s_af = sem("ln_affine")

        def layer_norm(block, it, width, pieces, dst, shape, gb=None, plain=None, ready=None, free=None, early=None):
            def done(k):
                return it * CH + k + 1

            @block.tensor
            def _(pe):
                def variance(k):
                    pe.wait_ge(s_sq, done(k))
                    if k >= 2:
                        pe.wait_ge(s_rs, done(k - 2))
                    pe.matmul(banks[4 + k % 2][:, 0:width], mean[:, :], sq[:, k % 2, 0:width],
                              start=True, stop=True).then_inc(s_var, 1)

                for k in range(CH):
                    if ready:
                        ready(pe, k)
                    if k >= 4:
                        pe.wait_ge(s_xn, done(k - 4))
                    parts = pieces(k, banks[k % 4][:, 0:width])
                    for n, (o, src) in enumerate(parts):
                        last = pe.matmul(o, centre[:, :], src, start=True, stop=True)
                    last.then_inc(s_xc, 1)
                    if k:
                        variance(k - 1)
                variance(CH - 1)

            @block.scalar
            def _(act):
                act.activation(junk[:, :], junk[:, :], ACT.Abs_reciprocal_sqrt)

                def rstd(k):
                    act.wait_ge(s_var, done(k))
                    if k >= 2:
                        act.wait_ge(s_xn, done(k - 2))
                    act.activation(rs[:, k % 2, 0:width], banks[4 + k % 2][:, 0:width],
                                   ACT.Abs_reciprocal_sqrt, bias=eps[:, :]).then_inc(s_rs, 1)

                for k in range(CH):
                    act.wait_ge(s_xc, done(k))
                    if k >= 2:
                        act.wait_ge(s_var, done(k - 2))
                    act.activation(sq[:, k % 2, 0:width], banks[k % 4][:, 0:width], ACT.Square)\
                        .then_inc(s_sq, 1)
                    if k:
                        rstd(k - 1)
                rstd(CH - 1)

            @block.vector
            def _(dve):
                def affine(k):
                    dve.wait_ge(s_xn, done(k))
                    v = (plain or dst)(k)
                    dve.tensor_scalar(v, v, gb[0], gb[1], ALU.mult, ALU.add).then_inc(s_af, 1)

                for k in range(CH):
                    if early:
                        early(dve, k)
                    if k == 0 and free:
                        free(dve)
                    dve.wait_ge(s_rs, done(k))
                    dve.tensor_tensor(dst(k), shape(banks[k % 4][:, 0:width]), shape(rs[:, k % 2, 0:width]),
                                      ALU.mult).then_inc(s_xn, 1)
                    if k and gb is not None:
                        affine(k - 1)
                if gb is not None:
                    affine(CH - 1)

        def flat(v):
            return v

        def windows(v):
            return v.rearrange("p (row win c) -> p win row c", row=WS, win=NW)

        s_hi = sem("split_high")
        s_lo = sem("split_low")

        def split_chunk(dve, it, k, width, used):
            used()
            x = XN[:, k * width:(k + 1) * width]
            for h in range(2):
                r0, r1 = h * C, (h + 1) * C
                last = dve.tensor_copy(xs[r0:r1, k % 2, h, 0:width], x[r0:r1, :])
            last.then_inc(s_hi, 1)
            dve.wait_ge(s_hi, it * CH + k + 1)
            for h in range(2):
                r0, r1 = h * C, (h + 1) * C
                o = xs[C - r0:2 * C - r0, k % 2, h, 0:width]
                last = dve.tensor_tensor(o, x[r0:r1, :], xs[r0:r1, k % 2, h, 0:width].bitcast(F32), ALU.subtract)
            last.then_inc(s_lo, 1)

        def exact(pe, out, wh, wl, moving):
            pe.matmul(out, wh, moving, start=True, stop=False)
            return pe.matmul(out, wl, moving, start=False, stop=True)

        s_w1h = sem("w1_high")
        s_w1l = sem("w1_low")

        def split_weights(dve, n, w):
            dve.tensor_copy(w1p[:, 0, :], w).then_inc(s_w1h, 1)
            dve.wait_ge(s_w1h, n + 1)
            dve.tensor_tensor(w1p[:, 1, :], w, w1p[:, 0, :].bitcast(F32), ALU.subtract).then_inc(s_w1l, 1)

        s_up = sem("ff_up")
        s_ge = sem("ff_gelu")
        s_dn = sem("ff_down")
        s_fr = sem("ff_residual")

        def early_splits(it, width, affs):
            def early(dve, k):
                if k in (CH - 3, CH - 1):
                    n = (k - (CH - 3)) // 2
                    dve.wait_ge(s_af, affs * CH + n + 1)
                    split_chunk(dve, it, n, width, lambda: None)
            return early

        def feed_forward(block, it, p, width, base, w2, f1, f2, norms, affs):
            def done(n, k):
                return it * (CH * n) + k + 1

            @block.tensor
            def _(pe):
                def up(k):
                    pe.wait_ge(s_lo, done(1, k))
                    for u in range(4):
                        n = 4 * k + u
                        if n >= 4:
                            pe.wait_ge(s_ge, done(4, n - 4))
                        else:
                            pe.wait_ge(s_xn, norms * CH + 5 + n)
                        h, j = divmod(u, 2)
                        exact(pe, banks[u][:, 0:width], w1p[:, 0, j * P:(j + 1) * P],
                              w1p[:, 1, j * P:(j + 1) * P], xs[:, k % 2, h, 0:width]).then_inc(s_up, 1)

                def down(k):
                    pe.wait_ge(s_ge, done(4, 4 * k + 3))
                    if k >= 2:
                        pe.wait_ge(s_fr, done(1, k - 2))
                    for j in range(2):
                        for h in range(2):
                            last = pe.matmul(banks[4 + k % 2][h * C:(h + 1) * C, 0:width],
                                             w2[:, j * C:(j + 1) * C], hid[:, 4 * (k % 2) + 2 * h + j, 0:width],
                                             start=(j == 0), stop=(j == 1))
                    last.then_inc(s_dn, 1)

                for k in range(CH):
                    up(k)
                    if k:
                        down(k - 1)
                down(CH - 1)

            @block.scalar
            def _(act):
                for k in range(CH):
                    for u in range(4):
                        act.wait_ge(s_up, done(4, 4 * k + u))
                        if k >= 2 and u == 0:
                            act.wait_ge(s_dn, done(1, k - 2))
                        act.activation(hid[:, 4 * (k % 2) + u, 0:width], banks[u][:, 0:width], ACT.Gelu,
                                       bias=f1[:, u % 2:u % 2 + 1]).then_inc(s_ge, 1)

            @block.vector
            def _(dve):
                def used(k):
                    if k >= 2:
                        dve.wait_ge(s_up, done(4, 4 * (k - 2) + 3))

                for k in range(CH + 1):
                    if 1 <= k < CH - 1:
                        if k == 1:
                            dve.wait_ge(s_af, affs * CH + CH)
                        split_chunk(dve, it, k + 1, width, lambda: used(k + 1))
                    if k:
                        dve.wait_ge(s_dn, done(1, k - 1))
                        x = xcols(p, base + (k - 1) * width, width)
                        dve.scalar_tensor_tensor(x, banks[4 + (k - 1) % 2][:, 0:width], f2, x, ALU.add, ALU.add)\
                            .then_inc(s_fr, 1)

        with ExitStack() as tok:
            def sbt(name, shape, dt=F32):
                return tok.enter_context(nc.sbuf_tensor(name, shape, dt))

            GROUP, PIX = 4, 2 * PATCH * PATCH
            patches = KS[:, 0:TOK]
            pe_w = sbt("pe_w", [P, P])
            pe_v = sbt("pe_v", [P, 3])
            rel = sbt("rel", [P, 2 * STRIP])
            s_pin = sem("pe_loaded")
            s_pw = sem("pe_weights")
            s_pc = sem("pe_conv")
            s_pe = sem("pe_stored")
            s_rel = sem("rel_loaded")
            s_rz = sem("rel_cleared")
            with nc.Block() as block:
                @block.sync
                def _(sp):
                    sp.dma_start(pe_w[:, :], t["pe_w"]).then_inc(s_pw, 16)
                    sp.dma_start(pe_v[:, :], t["pe_v"]).then_inc(s_pw, 16)
                    sp.wait_ge(s_pw, 32)

                @block.vector
                def _(dve):
                    dve.memset(rel[:, :], 0.0).then_inc(s_rz, 1)
            with nc.Fori(0, PAIRS // GROUP) as q:
                with nc.Block() as block:
                    @block.sync
                    def _(sp):
                        sp.dma_start(patches, t["patches"][bass.ds(q, 1), :, :].rearrange("a k n -> k (a n)"))\
                            .then_inc(s_pin, 16)
                        for n in range(WIN):
                            ni, nj = divmod(n, WS)
                            src = t["rpb_rev"][bass.ds(q, 1), :, WS - 1 - ni:2 * WS - 1 - ni, WS - 1 - nj:2 * WS - 1 - nj]
                            dst = rel[n:n + 1, bass.ds(q * STRIP, STRIP)].rearrange("p (h a b) -> p h a b", h=HEADS, a=WS)
                            sp.dma_start(dst, src).then_inc(s_rel, 16)

                    for j in range(GROUP):
                        p = q * GROUP + j

                        @block.tensor
                        def _(pe):
                            if j == 0:
                                pe.wait_ge(s_pin, q * 16 + 16)
                            for k in range(CH):
                                if k >= 4:
                                    pe.wait_ge(s_pe, p * CH + k - 3)
                                elif j:
                                    pe.wait_ge(s_xn, (p - 1) * CH + 5 + k)
                                pe.matmul(banks[k % 4][:, 0:STRIP], pe_w[j * PIX:(j + 1) * PIX, :],
                                          patches[j * PIX:(j + 1) * PIX, k * STRIP:(k + 1) * STRIP],
                                          start=True, stop=True).then_inc(s_pc, 1)

                        @block.scalar
                        def _(act):
                            for k in range(CH):
                                act.wait_ge(s_pc, p * CH + k + 1)
                                act.activation(xcols(p, k * STRIP, STRIP), banks[k % 4][:, 0:STRIP], ACT.Identity,
                                               bias=pe_v[:, 0:1]).then_inc(s_pe, 1)

                        layer_norm(block, p, STRIP, lambda k, o: [(o, xcols(p, k * STRIP, STRIP))],
                                   lambda k: xcols(p, k * STRIP, STRIP), flat, (pe_v[:, 1:2], pe_v[:, 2:3]),
                                   ready=lambda pe, k: pe.wait_ge(s_pe, p * CH + min(k + 5, CH)))

            with nc.Block() as block:
                @block.sync
                def _(sp):
                    sp.wait_ge(s_rel, 2 * WIN * 16)
                    sp.dma_start(rel[C:C + WIN, :], rel[0:WIN, :]).then_inc(s_rel, 16)
                    sp.wait_ge(s_rel, 2 * WIN * 16 + 16)

            tw = sbt("tw", [P, TW_N])
            tv = sbt("tv", [P, TV_N])
            bias = sbt("bias", [P, 4, HEADS * WIN])
            amask = sbt("amask", [P, 4, WIN])
            headmask = sbt("headmask", [P, HEADS])
            stack = sbt("stack", [P, WIN])
            flat_hid = hid[:, :, :].rearrange("p a n -> p (a n)")
            qbd = KS[:, 0:2 * NW * P].rearrange("p (s a n) -> p s a n", s=2, a=NW)
            ksb = KS[:, 2 * NW * P:2 * NW * P + 2 * STRIP].rearrange("p (s n) -> p s n", s=2)
            kbd = flat_hid[:, 0:4 * STRIP].rearrange("p (s h n) -> p s h n", s=4, h=HEADS)
            probT = flat_hid[:, 4 * STRIP:4 * STRIP + 8 * P].rearrange("p (s a n) -> p s a n", s=2, a=4)
            osb = flat_hid[:, 4 * STRIP + 8 * P:5 * STRIP + 8 * P]
            ssb = sbt("ssb", [P, 3, HEADS, WIN])
            smax = sbt("smax", [P, 3, HEADS])
            prob = sbt("prob", [P, 3, HEADS, C])
            vb = sbt("vb", [P, 8, 2, HEADS, HD + 1])
            rcp = sbt("rcp", [P, 2, HEADS])
            on = sbt("on", [P, 2, C])
            psb = sbt("psb", [P, STRIP])
            s_tc = sem("swin_cleared")
            s_tl = sem("swin_loaded")
            s_bt = sem("swin_bias")
            sa = {n: sem("att_" + n) for n in (
                "q", "k", "qev", "kev", "kbd", "v", "s", "add", "max", "sub", "exp", "t", "tev", "vev", "av",
                "rcp", "nrm", "ot", "oev", "pj", "pev")}
            s_res = {n: sem(f"att_residual_{n}") for n in (0, SHIFT)}
            NG = NW * NW

            with nc.Block() as block:
                @block.vector
                def _(dve):
                    for m in (qbd[:, :, :, :], prob[:, :, :, :], bias[:, :, :]):
                        dve.memset(m, 0.0).then_inc(s_tc, 1)
                    dve.memset(vb[:, :, :, :, :], 1.0).then_inc(s_tc, 1)

                @block.gpsimd
                def _(pool):
                    pool.wait_ge(s_tc, 4)
                    v = vb[:, :, :, :, :].rearrange("p a w (j e) d -> p (a w j) e d", e=2)
                    pool.memset(v[0:C, :, 1, :], 0.0).then_inc(s_tc, 1)
                    pool.memset(v[C:P, :, 0, :], 0.0).then_inc(s_tc, 1)

                @block.sync
                def _(sp):
                    sp.dma_start(headmask[:, :], t["headmask"]).then_inc(s_tl, 16)
                    sp.dma_start(stack[:, :], t["stack"]).then_inc(s_tl, 16)
                    sp.wait_ge(s_tl, 32)

            def swin_load(layer):
                with nc.Block() as block:
                    @block.sync
                    def _(sp):
                        sp.dma_start(tw[:, :], t["tok_w"][layer, :, :]).then_inc(s_tl, 16)
                        sp.dma_start(tv[:, :], t["tok_v"][layer, :, :]).then_inc(s_tl, 16)
                        sp.dma_start(amask[:, :, :], t["amask"][layer, :, :, :]).then_inc(s_tl, 16)
                        sp.wait_ge(s_tl, 32 + (layer + 1) * 16 * 3)

                with nc.Block() as block:
                    @block.vector
                    def _(dve):
                        split_weights(dve, layer, tw[:, TW["w1"]:TW["w1"] + FF])
                        i = rel[:, layer * STRIP:(layer + 1) * STRIP].rearrange("p (h m) -> p h m", h=HEADS)
                        for kind in range(4):
                            o = bias[:, kind, :].rearrange("p (h m) -> p h m", h=HEADS)
                            dve.tensor_tensor(o, i, amask[:, kind, :].unsqueeze(1).broadcast_to([P, HEADS, WIN]),
                                              ALU.add).then_inc(s_bt, 1)

            def swin_attention(block, it, p, base, shift, affs):
                def at(kind, n, k):
                    return it * n + k + 1

                def residuals(s):
                    return p * (NW * NRES) + NRES * (s + 1)

                def strip_x(s):
                    x = xcols(p, base + s * STRIP, STRIP).rearrange("p (row c) -> p row c", row=WS)
                    w = psb[:, :].rearrange("p (win row c) -> p win row c", win=NW, row=WS)
                    if not shift:
                        return [(x.rearrange("p row (win c) -> p win row c", win=NW), w)]
                    m = (NW - 1) * WS
                    return [(x[:, :, shift:shift + m].rearrange("p row (win c) -> p win row c", win=NW - 1), w[:, 0:NW - 1, :, :]),
                            (x[:, :, shift + m:GRID], w[:, NW - 1, :, 0:WS - shift]),
                            (x[:, :, 0:shift], w[:, NW - 1, :, WS - shift:WS])]

                NRES = 3 if shift else 1
                SLOTS = NG + 10

                @block.tensor
                def _(pe):
                    for i in range(-NW + 1, SLOTS):
                        if 0 <= i < NG:
                            if i == 0:
                                pe.wait_ge(s_af, affs * CH + CH)
                            pe.wait_ge(sa["kbd"], at("kbd", NG, i))
                            if i % NW == 0:
                                pe.wait_ge(sa["qev"], at("qev", NW, i // NW))
                            if i >= 2:
                                pe.wait_ge(sa["add"], at("add", NG, i - 2))
                            pe.matmul(banks[1 + i % 2][:, 0:HEADS * WIN], qbd[:, (i // NW) % 2, i % NW, :],
                                      kbd[:, i % 4, :, :], start=True, stop=True).then_inc(sa["s"], 1)
                        g = i - 3
                        if 0 <= g < NG:
                            pe.wait_ge(sa["exp"], at("exp", NG, g))
                            if g >= 2:
                                pe.wait_ge(sa["tev"], at("tev", NG, g - 2))
                            for j in range(4):
                                last = pe.transpose(banks[3 + g % 2][:, j * P:(j + 1) * P],
                                                    prob[:, g % 3, 2 * j:2 * j + 2, :], ident[:, :])
                            last.then_inc(sa["t"], 1)
                        s, r = divmod(i + NW - 1, NW)
                        if r == 0 and s < NW:
                            if s == 0:
                                pe.wait_ge(s_af, affs * CH + 5)
                            if s >= 3:
                                pe.wait_ge(sa["pev"], at("pev", NW, s - 3))
                            pe.matmul(banks[0][:, 0:STRIP], tw[:, TW["q"]:TW["q"] + P],
                                      XN[:, s * STRIP:(s + 1) * STRIP], start=True, stop=True).then_inc(sa["q"], 1)
                        if r == 2 and s < NW:
                            pe.wait_ge(sa["qev"], at("qev", NW, s))
                            pe.matmul(banks[0][:, 0:STRIP], tw[:, TW["k"]:TW["k"] + P],
                                      XN[:, s * STRIP:(s + 1) * STRIP], start=True, stop=True).then_inc(sa["k"], 1)
                        s, r = divmod(i - NW - 6, NW)
                        if r == 0 and 0 <= s < NW:
                            pe.wait_ge(sa["oev"], at("oev", NW, s))
                            if s + 2 < NW:
                                pe.wait_ge(sa["kev"], at("kev", NW, s + 2))
                            else:
                                pe.wait_ge(sa["pev"], at("pev", NW, s - 1))
                            pe.matmul(banks[0][:, 0:STRIP], tw[:, TW["p"]:TW["p"] + P], osb,
                                      start=True, stop=True).then_inc(sa["pj"], 1)
                        if 0 <= i < NG and i % 4 == 1:
                            if i > 1:
                                pe.wait_ge(sa["vev"], at("vev", NG // 4, i // 4 - 1))
                            for n in range(4):
                                for e in range(2):
                                    last = pe.matmul(banks[5][e * C:(e + 1) * C, n * C:(n + 1) * C],
                                                     XN[:, (i - 1 + n) * WIN:(i - 1 + n) * WIN + C],
                                                     tw[:, TW["v"] + e * C:TW["v"] + (e + 1) * C],
                                                     start=True, stop=True)
                            last.then_inc(sa["v"], 1)
                        g = i - 4
                        if 0 <= g < NG:
                            pe.wait_ge(sa["tev"], at("tev", NG, g))
                            pe.wait_ge(sa["vev"], at("vev", NG // 4, g // 4))
                            if g > NW and g % NW == 1:
                                pe.wait_ge(sa["oev"], at("oev", NW, g // NW - 1))
                            if g:
                                pe.wait_ge(sa["nrm"], at("nrm", NG, g - 1))
                            for j in range(4):
                                a, b = 2 * j * (HD + 1), (2 * j + 2) * (HD + 1)
                                for h in range(2):
                                    v = vb[:, g % 8, h, :, :].rearrange("p h d -> p (h d)")
                                    last = pe.matmul(banks[6][h * C:(h + 1) * C, a:b],
                                                     probT[:, g % 2, j, h * C:(h + 1) * C], v[:, a:b],
                                                     start=True, stop=True)
                            last.then_inc(sa["av"], 1)
                        g = i - 5
                        if 0 <= g < NG:
                            if g == NG - 1:
                                pe.wait_ge(sa["nrm"], at("nrm", NG, g))
                                pe.sem_inc(s_passed, 1)
                            for h in range(2):
                                r0, r1 = h * C, (h + 1) * C
                                last = pe.matmul(banks[7][r0:r1, (g % NW) * WIN:(g % NW + 1) * WIN],
                                                 on[r0:r1, g % 2, :], stack[r0:r1, :], start=True, stop=True)
                            last.then_inc(sa["ot"], 1)

                @block.scalar
                def _(act):
                    for i in range(-NW + 1, SLOTS):
                        g = i - 1
                        if 0 <= g < NG:
                            act.wait_ge(sa["sub"], at("sub", NG, g))
                            if g >= 3:
                                act.wait_ge(sa["t"], at("t", NG, g - 3))
                            act.activation(prob[:, g % 3, :, 0:WIN], ssb[:, g % 3, :, :], ACT.Exp)\
                                .then_inc(sa["exp"], 1)
                        s, r = divmod(i - NW - 5, NW)
                        if r == 0 and 0 <= s < NW:
                            act.wait_ge(sa["ot"], at("ot", NG, NW * s + NW - 1))
                            if s:
                                act.wait_ge(sa["pj"], at("pj", NW, s - 1))
                            act.activation(osb, banks[7][:, 0:STRIP], ACT.Identity,
                                           bias=tv[:, TV["v"]:TV["v"] + 1]).then_inc(sa["oev"], 1)
                        g = i - 3
                        if 0 <= g < NG:
                            act.wait_ge(sa["t"], at("t", NG, g))
                            if g >= 2:
                                act.wait_ge(sa["av"], at("av", NG, g - 2))
                            act.activation(probT[:, g % 2, :, :].rearrange("p a b -> p (a b)"), banks[3 + g % 2][:, :],
                                           ACT.Copy).then_inc(sa["tev"], 1)
                        s, r = divmod(i + NW - 1, NW)
                        if r == 0 and s < NW:
                            act.wait_ge(sa["q"], at("q", NW, s))
                            if s >= 2:
                                act.wait_ge(sa["s"], at("s", NG, NW * (s - 1) - 1))
                            for h in range(2):
                                r0, r1 = h * C, (h + 1) * C
                                last = act.activation(
                                    qbd[r0:r1, s % 2, :, r0:r0 + WIN],
                                    banks[0][r0:r1, 0:STRIP].rearrange("p (win n) -> p win n", win=NW),
                                    ACT.Identity, bias=tv[r0:r1, TV["q"]:TV["q"] + 1])
                            last.then_inc(sa["qev"], 1)
                        if r == 2 and s < NW:
                            act.wait_ge(sa["k"], at("k", NW, s))
                            if s >= 2:
                                act.wait_ge(sa["kbd"], at("kbd", NG, NW * (s - 1) - 1))
                            act.activation(ksb[:, s % 2, :], banks[0][:, 0:STRIP], ACT.Identity,
                                           bias=tv[:, TV["k"]:TV["k"] + 1]).then_inc(sa["kev"], 1)
                        s, r = divmod(i - NW - 6, NW)
                        if r == 0 and 0 <= s < NW:
                            act.wait_ge(sa["pj"], at("pj", NW, s))
                            if s:
                                act.wait_ge(s_res[shift], residuals(s - 1))
                            act.activation(psb[:, :], banks[0][:, 0:STRIP], ACT.Identity,
                                           bias=tv[:, TV["p"]:TV["p"] + 1]).then_inc(sa["pev"], 1)

                @block.vector
                def _(dve):
                    for i in range(SLOTS):
                        if i < NG:
                            dve.wait_ge(sa["s"], at("s", NG, i))
                            if i >= 3:
                                dve.wait_ge(sa["exp"], at("exp", NG, i - 3))
                            kind = 2 * (i // NW == NW - 1) + (i % NW == NW - 1) if shift else 0
                            sv = ssb[:, i % 3, :, :]
                            dve.scalar_tensor_tensor(sv.rearrange("p h m -> p (h m)"), banks[1 + i % 2][:, 0:HEADS * WIN],
                                                     QSCALE, bias[:, kind, :], ALU.mult, ALU.add)\
                                .then_inc(sa["add"], 1)
                            dve.wait_ge(sa["add"], at("add", NG, i))
                            dve.tensor_reduce(smax[:, i % 3, :], sv, op=ALU.max, axis=AX.X).then_inc(sa["max"], 1)
                        g = i - 4
                        if 0 <= g < NG:
                            dve.wait_ge(sa["av"], at("av", NG, g))
                            av = banks[6][:, 0:HEADS * (HD + 1)].rearrange("p (h d) -> p h d", h=HEADS)
                            dve.reciprocal(rcp[:, g % 2, :], av[:, :, HD]).then_inc(sa["rcp"], 1)
                            dve.wait_ge(sa["rcp"], at("rcp", NG, g))
                            if g >= 2:
                                dve.wait_ge(sa["ot"], at("ot", NG, g - 2))
                            dve.tensor_tensor(on[:, g % 2, :].rearrange("p (h d) -> p h d", d=HD), av[:, :, 0:HD],
                                              rcp[:, g % 2, :].unsqueeze(2).broadcast_to([P, HEADS, HD]),
                                              ALU.mult).then_inc(sa["nrm"], 1)
                        if i < NG and i % 4 == 1:
                            n = i // 4
                            dve.wait_ge(sa["v"], at("v", NG // 4, n))
                            if n >= 2:
                                dve.wait_ge(sa["av"], at("av", NG, 4 * n - 5))
                            for e in range(2):
                                r0, r1 = e * C, (e + 1) * C
                                o = vb[r0:r1, 4 * (n % 2):4 * (n % 2) + 4, :, :, 0:HD]\
                                    .rearrange("p a w (j e) d -> p (a w j) e d", e=2)
                                v = banks[5][r0:r1, 0:4 * C].rearrange("p (x d) -> p x d", d=HD)
                                last = dve.tensor_copy(o[:, :, e, :], v)
                            last.then_inc(sa["vev"], 1)

                @block.gpsimd
                def _(pool):
                    for i in range(-2, SLOTS):
                        g = i + 2
                        if 0 <= g < NG:
                            if g % NW == 0:
                                pool.wait_ge(sa["kev"], at("kev", NW, g // NW))
                            if g >= 4:
                                pool.wait_ge(sa["s"], at("s", NG, g - 4))
                            k = ksb[:, (g // NW) % 2, (g % NW) * WIN:(g % NW + 1) * WIN]
                            pool.tensor_tensor(kbd[:, g % 4, :, :], k.unsqueeze(1).broadcast_to([P, HEADS, WIN]),
                                               headmask[:, :].unsqueeze(2).broadcast_to([P, HEADS, WIN]), ALU.mult)\
                                .then_inc(sa["kbd"], 1)
                        if 0 <= i < NG:
                            pool.wait_ge(sa["max"], at("max", NG, i))
                            pool.tensor_tensor(ssb[:, i % 3, :, :], ssb[:, i % 3, :, :],
                                               smax[:, i % 3, :].unsqueeze(2).broadcast_to([P, HEADS, WIN]),
                                               ALU.subtract).then_inc(sa["sub"], 1)
                        s, r = divmod(i - NW - 6, NW)
                        if r == 0 and 0 <= s < NW:
                            pool.wait_ge(sa["pev"], at("pev", NW, s))
                            for x, w in strip_x(s):
                                pool.tensor_tensor(x, x, w, ALU.add).then_inc(s_res[shift], 1)

            def rolled(p, shift):
                def pieces(k, o):
                    x = xcols(p, shift * GRID + k * STRIP, STRIP)
                    if not shift:
                        return [(o, x)]
                    x = x.rearrange("p (row c) -> p row c", row=WS)
                    o = o.rearrange("p (row c) -> p row c", row=WS)
                    return [(o[:, :, 0:GRID - shift], x[:, :, shift:GRID]), (o[:, :, GRID - shift:GRID], x[:, :, 0:shift])]
                return pieces

            s_cp = sem("rows_copied")
            for layer, shift in enumerate((0, SHIFT)):
                swin_load(layer)
                base = shift * GRID
                if shift:
                    with nc.Block() as block:
                        @block.vector
                        def _(dve):
                            x = X[:, :].rearrange("p (a n) -> p a n", a=PAIRS)
                            dve.tensor_copy(x[:, :, TOK:TOK + base], x[:, :, 0:base]).then_inc(s_cp, 1)
                with nc.Fori(0, PAIRS) as p:
                    it = p + layer * PAIRS if layer else p
                    norms = p * 2 + PAIRS * (1 + 2 * layer)

                    def strip_added(pe, k):
                        if k == 0:
                            pe.wait_ge(sa["pev"], it * NW + NW)
                        pe.wait_ge(s_res[shift], (p * NW + k + 1) * (3 if shift else 1))

                    with nc.Block() as block:
                        layer_norm(block, norms, STRIP, rolled(p, shift),
                                   lambda k: XN[:, k * STRIP:(k + 1) * STRIP]
                                   .rearrange("p (win row c) -> p win row c", win=NW, row=WS),
                                   windows, (tv[:, TV["g1"]:TV["g1"] + 1], tv[:, TV["b1"]:TV["b1"] + 1]),
                                   plain=lambda k: XN[:, k * STRIP:(k + 1) * STRIP])
                        swin_attention(block, it, p, base, shift, norms)
                        layer_norm(block, norms + 1, STRIP, lambda k, o: [(o, xcols(p, base + k * STRIP, STRIP))],
                                   lambda k: XN[:, k * STRIP:(k + 1) * STRIP], flat,
                                   (tv[:, TV["g2"]:TV["g2"] + 1], tv[:, TV["b2"]:TV["b2"] + 1]),
                                   ready=strip_added, early=early_splits(p + layer * PAIRS, STRIP, norms + 1))
                        feed_forward(block, p + layer * PAIRS, p, STRIP, base,
                                     tw[:, TW["w2"]:TW["w2"] + 2 * C],
                                     tv[:, TV["f1"]:TV["f1"] + 2], tv[:, TV["f2"]:TV["f2"] + 1], norms + 1, norms + 1)

        s_tab = sem("positions_loaded")
        s_sp = sem("h_put_aside")
        s_pos = sem("positions_added")
        with nc.Block() as block:
            @block.sync
            def _(sp):
                sp.dma_start(KS[:, :], t["positions"]).then_inc(s_tab, 16)
                sp.dma_start(h_dram[PAIRS], t["positions"]).then_inc(s_tab, 16)
                sp.wait_ge(s_tab, 32)
        with nc.Fori(0, PAIRS) as p:
            with nc.Block() as block:
                @block.sync
                def _(sp):
                    sp.dma_start(h_dram[bass.ds(p, 1), :, :].rearrange("a k n -> k (a n)"), xcols(p, BASE, SEQP))\
                        .then_inc(s_sp, 16)
                    sp.wait_ge(s_sp, p * 16 + 16)
                    sp.sem_inc(s_arrived, 1)

                layer_norm(block, p + 5 * PAIRS, CW, lambda k, o: [(o, xcols(p, BASE + k * CW, CW))],
                           lambda k: xcols(p, BASE + k * CW, CW), flat, None,
                           free=lambda dve: dve.wait_ge(s_sp, p * 16 + 16))

                @block.gpsimd
                def _(pool):
                    for k in range(CH):
                        pool.wait_ge(s_xn, (p + 5 * PAIRS) * CH + k + 1)
                        x = xcols(p, BASE + k * CW, CW)
                        pool.tensor_tensor(x, x, KS[:, k * CW:(k + 1) * CW], ALU.add).then_inc(s_pos, 1)

        with ExitStack() as lin:
            def sbl(name, shape, dt=F32):
                return lin.enter_context(nc.sbuf_tensor(name, shape, dt))

            lw = sbl("lw", [P, LW_N])
            lv = sbl("lv", [P, LV_N])
            kmax = sbl("kmax", [P, CH])
            nkmax = sbl("nkmax", [P, 1])
            ksum = sbl("ksum", [P, CH])
            ksum1 = sbl("ksum1", [P, 1])
            rk = sbl("rk", [P, 1])
            ctm = sbl("ctm", [P, P])
            mix = sbl("mix", [P, P])
            kv = sbl("kv", [TT, 4, 2, 2 * P])
            qs = sbl("qs", [TT, 4, TPC * P])
            qm = sbl("qm", [TT, 2, TPC * 2 * HEADS])
            qd = sbl("qd", [TT, 2, TPC * 2 * HEADS])
            qr = sbl("qr", [TT, 2, TPC * 2 * HEADS])
            qT = sbl("qT", [P, 2, CW])
            hid_cols = hid[:, :, :].rearrange("p a n -> p (a n)")
            s_ll = sem("lin_loaded")
            s_z = sem("lin_cleared")
            sl = {n: sem("lin_" + n) for n in (
                "k", "max", "nmax", "exp", "sum", "rk", "kv", "kvev_act", "kvev_dve", "ctx", "mask", "mix", "mixev",
                "q", "pv", "qmax", "qsub", "qexp", "qsum", "qrcp", "qnrm", "qt", "qtev", "out", "res")}
            NQ = NT // 2
            LAYERS = 4

            with nc.Block() as block:
                @block.vector
                def _(dve):
                    dve.memset(KS[:, SEQ:SEQP], 0.0).then_inc(s_z, 1)
                    dve.memset(ctm[:, :], 0.0).then_inc(s_z, 1)

            def keys(block, it, affs):
                def valid(k):
                    return LAST if k == CH - 1 else CW

                @block.tensor
                def _(pe):
                    for k in range(CH):
                        pe.wait_ge(s_af, affs * CH + min(k + 5, CH))
                        pe.matmul(banks[k][:, 0:CW], lw[:, LW["k"]:LW["k"] + P], XN[:, k * CW:(k + 1) * CW],
                                  start=True, stop=True).then_inc(sl["k"], 1)

                @block.scalar
                def _(act):
                    act.wait_ge(sl["nmax"], it + 1)
                    for k in range(CH):
                        act.activation(KS[:, k * CW:k * CW + valid(k)], banks[k][:, 0:valid(k)], ACT.Exp,
                                       bias=nkmax[:, :], accum_out=ksum[:, k:k + 1]).then_inc(sl["exp"], 1)

                @block.vector
                def _(dve):
                    for k in range(CH):
                        dve.wait_ge(sl["k"], it * CH + k + 1)
                        dve.tensor_reduce(kmax[:, k:k + 1], banks[k][:, 0:valid(k)], op=ALU.max, axis=AX.X)\
                            .then_inc(sl["max"], 1)
                    dve.wait_ge(sl["max"], it * CH + CH)
                    dve.tensor_reduce(nkmax[:, :], kmax[:, :], op=ALU.max, axis=AX.X, negate=True)\
                        .then_inc(sl["nmax"], 1)

            def probs(k):
                if k < CH // 2:
                    return qs[:, k, :]
                return hid_cols[0:TT, (k - CH // 2) * TPC * P:(k - CH // 2 + 1) * TPC * P]

            def grouped_probs(k):
                return probs(k).rearrange("p (g d) -> p g d", d=HD)

            G = TPC * 2 * HEADS
            LAG = 3

            def chunk_at(i):
                k, r = divmod(i - LAG, 2)
                return k if r == 0 and 0 <= k < CH else None

            def context(block, it):
                QQ = NQ // 4

                def done(k):
                    return it * CH + k + 1

                def evacuated(i):
                    if i % 4 == 1:
                        return sl["kvev_dve"], it * QQ + i // 4 + 1
                    return sl["kvev_act"], it * (NQ - QQ) + i - (i + 2) // 4 + 1

                @block.tensor
                def _(pe):
                    for i in range(NQ + LAG):
                        k = chunk_at(i)
                        if k is not None:
                            if k >= 2:
                                pe.wait_ge(sl["qsub"], done(k - 2))
                            else:
                                pe.wait_ge(sl["exp"], it * CH + 7 + k)
                            for n in range(TPC):
                                a = k * CW + n * TT
                                last = pe.matmul(banks[6 + k % 2][0:TT, n * P:(n + 1) * P], XN[:, a:a + TT],
                                                 lw[:, LW["q"]:LW["q"] + P], start=True, stop=True)
                            last.then_inc(sl["q"], 1)
                        if i < NQ:
                            if i >= 4:
                                pe.wait_ge(*evacuated(i - 4))
                            pe.wait_ge(sl["exp"], it * CH + (i if i < 4 else i // 2) + 1)
                            b = banks[i % 4]
                            for n in range(2):
                                a = (2 * i + n) * TT
                                pe.transpose(b[0:TT, n * 2 * P:n * 2 * P + P], KS[:, a:a + TT], ident[:, :])
                                last = pe.matmul(b[0:TT, n * 2 * P + P:(n + 1) * 2 * P], XN[:, a:a + TT],
                                                 lw[:, LW["v"]:LW["v"] + P], start=True, stop=True)
                            last.then_inc(sl["kv"], 1)
                        g = i - LAG
                        if g >= 0:
                            if g == 0:
                                pe.wait_ge(sl["exp"], it * CH + 5)
                            pe.wait_ge(*evacuated(g))
                            for n in range(2):
                                for h in range(2):
                                    r0, r1 = h * C, (h + 1) * C
                                    last = pe.matmul(banks[4][r0:r1, 0:C], kv[:, g % 4, n, P + r0:P + r1],
                                                     kv[:, g % 4, n, r0:r1],
                                                     start=(g == 0 and n == 0), stop=(g == NQ - 1 and n == 1))
                            last.then_inc(sl["ctx"], 1)

                def evacuate(i):
                    return kv[:, i % 4, :, :].rearrange("p a b -> p (a b)"), banks[i % 4][0:TT, :]

                @block.scalar
                def _(act):
                    for i in range(NQ + LAG):
                        if i < NQ and i % 4 != 1:
                            act.wait_ge(sl["kv"], it * NQ + i + 1)
                            if i >= 4:
                                act.wait_ge(sl["ctx"], it * NQ + i - 3)
                            o, b = evacuate(i)
                            act.activation(o, b, ACT.Copy).then_inc(sl["kvev_act"], 1)
                        k = chunk_at(i)
                        if k is not None:
                            act.wait_ge(sl["qsub"], done(k))
                            act.activation(probs(k), probs(k), ACT.Exp).then_inc(sl["qexp"], 1)

                @block.vector
                def _(dve):
                    def normaliser(k):
                        dve.wait_ge(sl["qexp"], done(k))
                        dve.tensor_reduce(qd[:, k % 2, :], grouped_probs(k), op=ALU.add, axis=AX.X)\
                            .then_inc(sl["qsum"], 1)
                        if k >= 2:
                            dve.wait_ge(sl["qnrm"], done(k - 2))
                        dve.wait_ge(sl["qsum"], done(k))
                        dve.reciprocal(qr[:, k % 2, :], qd[:, k % 2, :]).then_inc(sl["qrcp"], 1)

                    for i in range(NQ + LAG):
                        k = chunk_at(i)
                        if k is not None:
                            dve.wait_ge(sl["q"], done(k))
                            b = banks[6 + k % 2][0:TT, :].rearrange("p (g d) -> p g d", d=HD)
                            dve.tensor_reduce(qm[:, k % 2, :], b, op=ALU.max, axis=AX.X).then_inc(sl["qmax"], 1)
                            dve.wait_ge(sl["qmax"], done(k))
                            dve.tensor_tensor(grouped_probs(k), b,
                                              qm[:, k % 2, :].unsqueeze(2).broadcast_to([TT, G, HD]),
                                              ALU.subtract).then_inc(sl["qsub"], 1)
                        k = chunk_at(i - 2)
                        if k is not None:
                            normaliser(k)
                        if i < NQ and i % 4 == 1:
                            dve.wait_ge(sl["kv"], it * NQ + i + 1)
                            if i >= 4:
                                dve.wait_ge(sl["ctx"], it * NQ + i - 3)
                            o, b = evacuate(i)
                            dve.tensor_copy(o, b).then_inc(sl["kvev_dve"], 1)
                    dve.wait_ge(sl["ctx"], it * NQ + NQ)
                    for h in range(2):
                        r0, r1 = h * C, (h + 1) * C
                        last = dve.tensor_tensor(ctm[r0:r1, r0:r1], banks[4][r0:r1, 0:C], bdmask[r0:r1, r0:r1], ALU.mult)
                    last.then_inc(sl["mask"], 1)
                    dve.wait_ge(sl["exp"], it * CH + CH)
                    dve.tensor_reduce(ksum1[:, :], ksum[:, :], op=ALU.add, axis=AX.X).then_inc(sl["sum"], 1)
                    dve.wait_ge(sl["sum"], it + 1)
                    dve.reciprocal(rk[:, :], ksum1[:, :]).then_inc(sl["rk"], 1)
                    dve.wait_ge(sl["rk"], it + 1)
                    dve.wait_ge(sl["mix"], it + 1)
                    dve.tensor_scalar(mix[:, :], banks[5][:, 0:P], rk[:, :], QSCALE, ALU.mult, ALU.mult)\
                        .then_inc(sl["mixev"], 1)
                    normaliser(CH - 1)

                @block.gpsimd
                def _(pool):
                    for k in range(CH):
                        pool.wait_ge(sl["qrcp"], done(k))
                        pool.tensor_tensor(grouped_probs(k), grouped_probs(k),
                                           qr[:, k % 2, :].unsqueeze(2).broadcast_to([TT, G, HD]), ALU.mult)\
                            .then_inc(sl["qnrm"], 1)

            def queries(block, it, p):
                def done(k):
                    return it * CH + k + 1

                def product(k):
                    a = CH // 2 * TPC * P + (k % 2) * CW
                    return hid_cols[:, a:a + CW]

                @block.tensor
                def _(pe):
                    for i in range(CH + 2):
                        if i < CH:
                            pe.wait_ge(sl["qnrm"], done(i))
                            if i >= 2:
                                pe.wait_ge(sl["qtev"], done(i - 2))
                            for n in range(TPC):
                                last = pe.transpose(banks[i % 2][:, n * TT:(n + 1) * TT],
                                                    probs(i)[:, n * P:(n + 1) * P], ident[0:TT, 0:TT])
                            last.then_inc(sl["qt"], 1)
                        if i == 0:
                            pe.wait_ge(sl["mask"], it + 1)
                            pe.matmul(banks[5][:, 0:P], ctm[:, :], lw[:, LW["o"]:LW["o"] + P], start=True, stop=True)\
                                .then_inc(sl["mix"], 1)
                        k = i - 2
                        if k >= 0:
                            pe.wait_ge(sl["qtev"], done(k))
                            if k >= 2:
                                pe.wait_ge(sl["pv"], done(k - 2))
                            if k == 0:
                                pe.wait_ge(sl["mixev"], it + 1)
                            pe.matmul(banks[2 + k % 2][:, 0:CW], mix[:, :], qT[:, k % 2, :],
                                      start=True, stop=True).then_inc(sl["out"], 1)

                @block.scalar
                def _(act):
                    for i in range(CH + 2):
                        if i < CH:
                            act.wait_ge(sl["qt"], done(i))
                            if i >= 2:
                                act.wait_ge(sl["out"], done(i - 2))
                            act.activation(qT[:, i % 2, :], banks[i % 2][:, 0:CW], ACT.Copy).then_inc(sl["qtev"], 1)
                        k = i - 2
                        if k >= 0:
                            act.wait_ge(sl["out"], done(k))
                            if k >= 2:
                                act.wait_ge(sl["res"], done(k - 2))
                            act.activation(product(k), banks[2 + k % 2][:, 0:CW], ACT.Identity,
                                           bias=lv[:, LV["o"]:LV["o"] + 1]).then_inc(sl["pv"], 1)

                @block.gpsimd
                def _(pool):
                    for k in range(CH):
                        pool.wait_ge(sl["pv"], done(k))
                        x = xcols(p, BASE + k * CW, CW)
                        pool.tensor_tensor(x, x, product(k), ALU.add).then_inc(sl["res"], 1)

            with nc.Fori(0, LAYERS) as l:
                with nc.Block() as block:
                    @block.sync
                    def _(sp):
                        sp.dma_start(lw[:, :], t["lin_w"][bass.ds(l, 1), :, :].rearrange("a k n -> k (a n)"))\
                            .then_inc(s_ll, 16)
                        sp.dma_start(lv[:, :], t["lin_v"][bass.ds(l, 1), :, :].rearrange("a k n -> k (a n)"))\
                            .then_inc(s_ll, 16)
                        sp.wait_ge(s_ll, l * 32 + 32)
                        sp.sem_inc(s_arrived, 1)

                    @block.vector
                    def _(dve):
                        dve.wait_ge(s_ll, l * 32 + 32)
                        split_weights(dve, l + 2, lw[:, LW["w1"]:LW["w1"] + FF])
                with nc.Fori(0, PAIRS) as p:
                    it = l * PAIRS + p
                    stream = lambda k, o: [(o, xcols(p, BASE + k * CW, CW))]
                    normal = lambda k: XN[:, k * CW:(k + 1) * CW]
                    norms = it * 2 + 6 * PAIRS
                    affs = it * 2 + 5 * PAIRS

                    def chunk_added(pe, k):
                        pe.wait_ge(sl["res"], it * CH + (k + 1 if k < 2 else min(k + 5, CH)))

                    with nc.Block() as block:
                        layer_norm(block, norms, CW, stream, normal, flat,
                                   (lv[:, LV["g1"]:LV["g1"] + 1], lv[:, LV["b1"]:LV["b1"] + 1]))
                        keys(block, it, affs)
                        context(block, it)
                        queries(block, it, p)
                        layer_norm(block, norms + 1, CW, stream, normal, flat,
                                   (lv[:, LV["g2"]:LV["g2"] + 1], lv[:, LV["b2"]:LV["b2"] + 1]), ready=chunk_added,
                                   early=early_splits(it + 2 * PAIRS, CW, affs + 1))
                        feed_forward(block, it + 2 * PAIRS, p, CW, BASE,
                                     lw[:, LW["w2"]:LW["w2"] + 2 * C],
                                     lv[:, LV["f1"]:LV["f1"] + 2], lv[:, LV["f2"]:LV["f2"] + 1], norms + 1, affs + 1)

        with ExitStack() as moe:
            def sbm(name, shape, dt=F32):
                return moe.enter_context(nc.sbuf_tensor(name, shape, dt))

            U = 2 * EXP
            W3 = 3 * U
            mw = sbm("mw", [P, MW_N])
            mv = sbm("mv", [P, MV_N])
            w1e = sbm("w1e", [P, 2, EXP * P], F32R)
            br = sbm("br", [TT, U])
            rank = sbm("rank", [TT, U])
            b2f = sbm("b2f", [W3, P])
            b2p = sbm("b2p", [W3, 3, P], BF16)
            sel = sbm("sel", [W3, U, P], BF16)
            lg = sbm("lg", [TT, NT, U])
            r1 = sbm("r1", [TT, NT, U])
            r2 = sbm("r2", [TT, NT, U])
            o1 = sbm("o1", [TT, NT, U])
            o2 = sbm("o2", [TT, NT, U])
            ws3 = sbm("ws3", [TT, NT + 2, 3, U], BF16)
            m1 = sbm("m1", [TT, NT * 2])
            m2 = sbm("m2", [TT, NT * 2])
            mr = sbm("mr", [TT, NT * 2])
            ed = sbm("ed", [TT, NT * 2])
            w1s = sbm("w1s", [TT, NT * 2])
            w2s = sbm("w2s", [TT, NT * 2])
            wT = sbm("wT", [W3, SEQP], BF16)
            identb = sbm("identb", [TT, TT], BF16)
            yb = sbm("yb", [P, 2, CW])
            ob = sbm("ob", [TT, 2, TPC * P])
            w1f = XN[:, 0:EXP * P]
            self32 = hid[0:W3, :, :].rearrange("p a n -> p (a n)")[:, 0:U * P].rearrange("p (u n) -> p u n", u=U)
            s_ml = sem("moe_loaded")
            s_b2 = sem("moe_b2_parts")
            s_wc = sem("moe_cleared")
            s_rh = sem("moe_h_back")
            s_ha = sem("moe_h_added")
            sm = {n: sem("moe_" + n) for n in (
                "logits", "step", "diff", "edge", "wt", "wtev", "up", "gelu", "bc", "gated", "down", "y", "yt", "yev",
                "out0", "out1")}

            with nc.Block() as block:
                @block.sync
                def _(sp):
                    for dst, name in ((mw[:, :], "moe_w"), (mv[:, :], "moe_v"), (br[:, :], "moe_br"),
                                      (rank[:, :], "rank"), (b2f[:, :], "moe_b2"), (self32, "sel"), (w1f, "moe_w1")):
                        sp.dma_start(dst, t[name]).then_inc(s_ml, 16)
                    sp.dma_start(KS[:, :], h_dram[0]).then_inc(s_rh, 16)
                    sp.sem_inc(sm["out0"], 16)
                    sp.sem_inc(sm["out1"], 16)
                    sp.wait_ge(s_ml, 7 * 16)

                @block.vector
                def _(dve):
                    dve.wait_ge(s_ml, 7 * 16)
                    dve.tensor_copy(w1e[:, 0, :], w1f).then_inc(s_w1h, 1)
                    dve.wait_ge(s_w1h, 7)
                    dve.tensor_tensor(w1e[:, 1, :], w1f, w1e[:, 0, :].bitcast(F32), ALU.subtract).then_inc(s_w1l, 1)
                    dve.tensor_copy(sel[:, :, :], self32).then_inc(s_wc, 1)
                    dve.tensor_copy(identb[:, :], ident[0:TT, 0:TT]).then_inc(s_wc, 1)
                    dve.memset(ws3[:, NT:NT + 2, :, :], 0.0).then_inc(s_wc, 1)
                    for n in range(3):
                        dve.tensor_copy(b2p[:, n, :], b2f[:, :]).then_inc(s_b2, 1)
                        if n < 2:
                            dve.wait_ge(s_b2, 2 * n + 1)
                            dve.tensor_tensor(b2f[:, :], b2f[:, :], b2p[:, n, :], ALU.subtract).then_inc(s_b2, 1)
                            dve.wait_ge(s_b2, 2 * n + 2)

            def route(block, it, affs):
                STEPS = 23

                @block.tensor
                def _(pe):
                    for n in range(NT):
                        if n % TPC == 0:
                            pe.wait_ge(s_af, affs * CH + max(n // TPC + 1, 5))
                        last = pe.matmul(banks[0][0:TT, n * U:(n + 1) * U], XN[:, n * TT:(n + 1) * TT],
                                         mw[:, MW["r"]:MW["r"] + U], start=True, stop=True)
                    last.then_inc(sm["logits"], 1)
                    pe.wait_ge(sm["step"], it * STEPS + STEPS)
                    for k in range(CH):
                        if k >= 2:
                            pe.wait_ge(sm["wtev"], it * CH + k - 1)
                        b = banks[1 + k % 2][:, :].bitcast(BF16)
                        parts = ws3[:, :, :, :].rearrange("p t a u -> p (t a u)")
                        for n in range(TPC):
                            a = (k * TPC + n) * W3
                            last = pe.transpose(b[:, n * P:n * P + TT], parts[:, a:a + P], identb[:, :])
                        last.then_inc(sm["wt"], 1)

                @block.scalar
                def _(act):
                    act.wait_ge(sm["diff"], it + 1)
                    act.activation(ed[:, :], ed[:, :], ACT.Exp).then_inc(sm["edge"], 1)
                    for k in range(CH):
                        act.wait_ge(sm["wt"], it * CH + k + 1)
                        b = banks[1 + k % 2][0:W3, :].bitcast(BF16).rearrange("p (n c) -> p n c", c=P)
                        act.activation(wT[:, k * CW:(k + 1) * CW].rearrange("p (n c) -> p n c", c=TT),
                                       b[:, 0:TPC, 0:TT], ACT.Copy).then_inc(sm["wtev"], 1)

                @block.vector
                def _(dve):
                    count = [0]

                    def then(ins):
                        count[0] += 1
                        ins.then_inc(sm["step"], 1)
                        if count[0] < STEPS:
                            dve.wait_ge(sm["step"], it * STEPS + count[0])

                    def grouped(v):
                        return v[:, :, :].rearrange("p t (h e) -> p (t h) e", h=2)

                    def each(v):
                        return v[:, :].unsqueeze(2).broadcast_to([TT, NT * 2, EXP])

                    def tiles(v):
                        return v[:, :].unsqueeze(1).broadcast_to([TT, NT, U])

                    def first_of(one, best):
                        then(dve.tensor_tensor(grouped(r1), grouped(lg), each(best), ALU.is_equal))
                        then(dve.tensor_tensor(r1[:, :, :], r1[:, :, :], tiles(rank), ALU.mult))
                        then(dve.tensor_reduce(mr[:, :], grouped(r1), op=ALU.max, axis=AX.X))
                        then(dve.tensor_tensor(grouped(one), grouped(r1), each(mr), ALU.is_equal))

                    dve.wait_ge(sm["logits"], it + 1)
                    then(dve.tensor_tensor(lg[:, :, :], banks[0][0:TT, :].rearrange("p (t u) -> p t u", u=U),
                                           tiles(br), ALU.add))
                    then(dve.tensor_reduce(m1[:, :], grouped(lg), op=ALU.max, axis=AX.X))
                    first_of(o1, m1)
                    then(dve.scalar_tensor_tensor(lg[:, :, :].rearrange("p t u -> p (t u)"),
                                                  o1[:, :, :].rearrange("p t u -> p (t u)"), TOPK_BIG,
                                                  lg[:, :, :].rearrange("p t u -> p (t u)"), ALU.mult, ALU.add))
                    then(dve.tensor_reduce(m2[:, :], grouped(lg), op=ALU.max, axis=AX.X))
                    first_of(o2, m2)
                    dve.tensor_tensor(ed[:, :], m2[:, :], m1[:, :], ALU.subtract).then_inc(sm["diff"], 1)
                    dve.wait_ge(sm["edge"], it + 1)
                    then(dve.tensor_scalar(w1s[:, :], ed[:, :], 1.0, None, ALU.add))
                    then(dve.reciprocal(w1s[:, :], w1s[:, :]))
                    then(dve.tensor_tensor(w2s[:, :], ed[:, :], w1s[:, :], ALU.mult))
                    then(dve.tensor_tensor(grouped(o1), grouped(o1), each(w1s), ALU.mult))
                    then(dve.tensor_tensor(grouped(o2), grouped(o2), each(w2s), ALU.mult))
                    then(dve.tensor_tensor(r2[:, :, :], o1[:, :, :], o2[:, :, :], ALU.add))
                    for n in range(3):
                        then(dve.tensor_copy(ws3[:, 0:NT, n, :], r2[:, :, :]))
                        if n < 2:
                            then(dve.tensor_tensor(r2[:, :, :], r2[:, :, :], ws3[:, 0:NT, n, :], ALU.subtract))
                    assert count[0] == STEPS, count[0]

            def out_pieces(k):
                if k < CH - 1:
                    return [(0, TPC, 0, TT, 1 + BASE + k * CW)]
                found, wrap = [], TOK - BASE
                for n in range(TPC):
                    f = k * CW + n * TT
                    for a, b, to in ((f, min(f + TT, wrap), 1 + BASE + f),
                                     (max(f, wrap), min(f + TT, TOK), 1 + max(f, wrap) - wrap),
                                     (max(f, TOK), min(f + TT, SEQ), 0)):
                        if a < b:
                            found.append((n, 1, a - f, b - a, to))
                return found

            def stores(k):
                return sum(2 * len(out_pieces(c)) for c in range(k % 2, k + 1, 2))

            def experts(block, it, p):
                def done(n, k):
                    return it * (CH * n) + k + 1

                def outs(k):
                    return 16 + it * (16 * stores(CH - 2 + k % 2)) + 16 * stores(k)

                def outs_before(k):
                    return 16 + it * (16 * stores(CH - 2 + k % 2))

                LAG = 4

                def store(queue, k, h):
                    v = ob[:, k % 2, :].rearrange("p (n h c) -> p n h c", n=TPC, h=2)
                    o = out[bass.ds(p + h * PAIRS if h else p, 1), :, :].rearrange("a n c -> (a n) c")
                    for n0, nn, q0, nq, to in out_pieces(k):
                        dst = o[to:to + nn * nq, :].rearrange("(n q) c -> q n c", n=nn)
                        queue.dma_start(dst, v[q0:q0 + nq, n0:n0 + nn, h, :]).then_inc(sm[f"out{k % 2}"], 16)

                @block.tensor
                def _(pe):
                    for i in range(CH * U + LAG + 2):
                        if i < CH * U:
                            k, u = divmod(i, U)
                            e, h = divmod(u, 2)
                            c = h * EXP + e
                            if u == 0:
                                pe.wait_ge(s_lo, (it + 6 * PAIRS) * CH + k + 1)
                            if i >= 2:
                                pe.wait_ge(sm["gelu"], done(U, i - 2))
                            exact(pe, banks[i % 2][:, 0:CW], w1e[:, 0, e * P:(e + 1) * P],
                                  w1e[:, 1, e * P:(e + 1) * P], xs[:, k % 2, h, :]).then_inc(sm["up"], 1)
                            if i == 0:
                                pe.wait_ge(sm["wtev"], it * CH + CH)
                            if i >= 2:
                                pe.wait_ge(sm["gated"], done(U, i - 2))
                            pe.matmul(banks[2 + i % 2][:, 0:CW], sel[:, c, :], wT[:, k * CW:(k + 1) * CW],
                                      start=True, stop=True).then_inc(sm["bc"], 1)
                        g = i - LAG
                        if 0 <= g < CH * U and g % 2 == 1:
                            k, u = divmod(g, U)
                            e = u // 2
                            d = banks[4 + k % 2]
                            if e == 0:
                                if k >= 2:
                                    pe.wait_ge(sm["y"], done(1, k - 2))
                                for n in range(3):
                                    pe.matmul(d[:, 0:CW], b2p[:, n, :], wT[:, k * CW:(k + 1) * CW],
                                              start=(n == 0), stop=False)
                            pe.wait_ge(sm["gated"], done(U, g))
                            for h in range(2):
                                last = pe.matmul(d[h * C:(h + 1) * C, 0:CW],
                                                 mw[:, MW["w2"] + e * C:MW["w2"] + (e + 1) * C],
                                                 hid[:, (g - 1 + h) % 8, :], start=False, stop=(e == EXP - 1))
                            last.then_inc(sm["down"], 1)
                        g = i - LAG - 1
                        if g >= 0 and g % U == U - 1 and g // U < CH:
                            k = g // U
                            pe.wait_ge(sm["y"], done(1, k))
                            if k >= 2:
                                pe.wait_ge(sm["yev"], done(1, k - 2))
                            for n in range(TPC):
                                last = pe.transpose(banks[6 + k % 2][0:TT, n * P:(n + 1) * P],
                                                    yb[:, k % 2, n * TT:(n + 1) * TT], ident[:, :])
                            last.then_inc(sm["yt"], 1)

                @block.scalar
                def _(act):
                    for i in range(CH * U + U):
                        if i < CH * U:
                            e = (i % U) // 2
                            act.wait_ge(sm["up"], done(U, i))
                            if i >= 8:
                                act.wait_ge(sm["down"], done(EXP, (i - 8) // 2))
                            act.activation(hid[:, i % 8, :], banks[i % 2][:, 0:CW], ACT.Gelu,
                                           bias=mv[:, MV["f1"] + e:MV["f1"] + e + 1]).then_inc(sm["gelu"], 1)
                        g = i - U
                        if g >= 0 and g % U == U - 1:
                            k = g // U
                            act.wait_ge(sm["yt"], done(1, k))
                            if k >= 2:
                                act.wait_ge(sm[f"out{k % 2}"], outs(k - 2))
                            else:
                                act.wait_ge(sm[f"out{k % 2}"], outs_before(k))
                            act.activation(ob[:, k % 2, :], banks[6 + k % 2][0:TT, :], ACT.Copy)\
                                .then_inc(sm["yev"], 1)
                            if k == CH - 1:
                                act.wait_ge(sm["yev"], done(1, k))
                                store(act, k, 1)

                @block.vector
                def _(dve):
                    def used(k):
                        if k >= 2:
                            dve.wait_ge(sm["up"], done(U, U * (k - 1) - 1))

                    for i in range(CH * U + LAG + 1):
                        if i < CH * U:
                            if i % U == 4 and 1 <= i // U < CH - 1:
                                split_chunk(dve, it + 6 * PAIRS, i // U + 1, CW, lambda: used(i // U + 1))
                            dve.wait_ge(sm["gelu"], done(U, i))
                            dve.wait_ge(sm["bc"], done(U, i))
                            v = hid[:, i % 8, :]
                            dve.tensor_tensor(v, v, banks[2 + i % 2][:, 0:CW], ALU.mult).then_inc(sm["gated"], 1)
                        g = i - LAG
                        if g >= 0 and g % U == U - 1:
                            k = g // U
                            dve.wait_ge(sm["down"], done(EXP, k * EXP + EXP - 1))
                            if k >= 2:
                                dve.wait_ge(sm["yt"], done(1, k - 2))
                            dve.tensor_tensor(yb[:, k % 2, :], banks[4 + k % 2][:, 0:CW],
                                              xcols(p, BASE + k * CW, CW), ALU.add).then_inc(sm["y"], 1)

                @block.sync
                def _(sp):
                    for k in range(CH):
                        sp.wait_ge(sm["yev"], done(1, k))
                        store(sp, k, 0)
                        if k < CH - 1:
                            store(sp, k, 1)

            with nc.Fori(0, PAIRS) as p:
                norms = p * 2 + 14 * PAIRS
                normal = lambda k: XN[:, k * CW:(k + 1) * CW]

                def h_added(pe, k):
                    pe.wait_ge(s_ha, p * CH + k + 1)

                def normalised(pe, k):
                    pe.wait_ge(s_xn, norms * CH + min(k + 6, CH))

                with nc.Block() as block:
                    @block.sync
                    def _(sp):
                        sp.wait_ge(s_ha, p * CH + CH)
                        sp.dma_start(KS[:, :], h_dram[bass.ds(p + 1, 1), :, :].rearrange("a k n -> k (a n)"))\
                            .then_inc(s_rh, 16)

                    @block.vector
                    def _(dve):
                        dve.wait_ge(s_rh, p * 16 + 16)
                        for k in range(CH):
                            x = xcols(p, BASE + k * CW, CW)
                            dve.tensor_tensor(x, x, KS[:, k * CW:(k + 1) * CW], ALU.add).then_inc(s_ha, 1)

                    layer_norm(block, norms, CW, lambda k, o: [(o, xcols(p, BASE + k * CW, CW))], normal, flat, None,
                               ready=h_added)
                    layer_norm(block, norms + 1, CW, lambda k, o: [(o, normal(k))], normal, flat,
                               (mv[:, MV["g"]:MV["g"] + 1], mv[:, MV["b"]:MV["b"] + 1]),
                               ready=normalised, early=early_splits(p + 6 * PAIRS, CW, p + 13 * PAIRS))
                    route(block, p, p + 13 * PAIRS)
                    experts(block, p, p)

            with nc.Block() as block:
                @block.sync
                def _(sp):
                    sp.wait_ge(s_rh, PAIRS * 16 + 16)
                    for k in (0, 1):
                        sp.wait_ge(sm[f"out{k}"], 16 + PAIRS * 16 * stores(CH - 2 + k))


def twice(a):
    return np.concatenate([a, a], axis=0)


def diagonal(a):
    o = np.zeros((2 * a.shape[0], 2 * a.shape[1]), a.dtype)
    o[:a.shape[0], :a.shape[1]] = a
    o[a.shape[0]:, a.shape[1]:] = a
    return o


def second(a):
    return np.concatenate([a[:P], a[P:]], axis=1)


def constants():
    c = {}
    one = np.ones((C, C), np.float32) / C
    c["mean"] = diagonal(one)
    c["centre"] = np.eye(P, dtype=np.float32) - c["mean"]
    c["ident"] = np.eye(P, dtype=np.float32)
    c["bdmask"] = np.kron(np.eye(P // HD, dtype=np.float32), np.ones((HD, HD), np.float32))
    c["headmask"] = twice(np.kron(np.eye(HEADS, dtype=np.float32), np.ones((HD, 1), np.float32)))
    stack = np.zeros((C, WIN), np.float32)
    stack[:WIN] = np.eye(WIN, dtype=np.float32)
    c["stack"] = twice(stack)
    region = np.zeros((2, WS), np.int32)
    region[1, WS - SHIFT:] = 1
    amask = np.zeros((2, P, 4, WIN), np.float32)
    for kind in range(4):
        lab = (region[kind // 2][:, None] * 2 + region[kind % 2][None, :]).reshape(-1)
        m = np.where(lab[:, None] != lab[None, :], -100.0, 0.0).astype(np.float32)
        for h in (0, C):
            amask[1, h:h + WIN, kind, :] = m
    c["amask"] = amask
    pos = np.arange(SEQ, dtype=np.float32)[:, None]
    div = np.exp(np.arange(0, C, 2, dtype=np.float32) * (-np.log(np.float32(10000.0)) / np.float32(C)))
    pe = np.zeros((SEQ, C), np.float32)
    pe[:, 0::2] = np.sin(pos * div)
    pe[:, 1::2] = np.cos(pos * div)
    f = np.arange(SEQ)
    row = np.where(f < TOK - BASE, 1 + BASE + f, 1 + f - (TOK - BASE))
    row[TOK] = 0
    table = np.zeros((C, SEQP), np.float32)
    table[:, :SEQ] = pe[row].T
    c["positions"] = twice(table)
    U = 2 * EXP
    c["rank"] = np.tile(np.arange(EXP, 0, -1, dtype=np.float32), (TT, 2))
    sel = np.zeros((3 * U, U, P), np.float32)
    for part in range(3):
        for u in range(U):
            sel[part * U + u, u, :] = 1.0
    c["sel"] = sel
    return c


def laid_out(i):
    a = {k: np.asarray(v) for k, v in i.items()}
    t = {}
    x = a["x"].reshape(2, PAIRS, GRID, PATCH, GRID, PATCH)
    t["patches"] = np.ascontiguousarray(x.transpose(1, 0, 3, 5, 2, 4)).reshape(PAIRS // 4, P, TOK)
    t["cls"] = twice(a["cls_tok"].reshape(C, 1))
    g = lambda n: a["L0_tok_" + n]
    t["pe_w"] = np.tile(diagonal(g("pe_w").reshape(C, PATCH * PATCH).T), (4, 1))
    t["pe_v"] = twice(np.stack([g("pe_b"), g("pe_ng"), g("pe_nb")], axis=1))
    w, v = [], []
    for l in range(2):
        qkv = g("qkv_w")[l].T
        wv = qkv[:, 2 * C:].reshape(C, HEADS // 2, 2, HD)
        by_head = [diagonal(wv[:, :, e, :].reshape(C, C // 2)) for e in range(2)]
        w.append(np.concatenate([diagonal(qkv[:, :C]), diagonal(qkv[:, C:2 * C]), *by_head,
                                 diagonal(g("proj_w")[l].T), twice(g("w1")[l].T), second(g("w2")[l].T)], axis=1))
        b = g("qkv_b")[l]
        f1 = g("b1")[l]
        cols = [g("n1g")[l], g("n1b")[l], b[:C], b[C:2 * C], b[2 * C:], g("proj_b")[l], g("n2g")[l], g("n2b")[l]]
        v.append(np.concatenate([twice(np.stack(cols, axis=1)), f1.reshape(2, P).T,
                                 twice(g("b2")[l][:, None])], axis=1))
    t["tok_w"], t["tok_v"] = np.stack(w), np.stack(v)
    n = 2 * WS - 1
    t["rpb_rev"] = np.ascontiguousarray(g("rpb")[:, ::-1, :].transpose(0, 2, 1)).reshape(2, HEADS, n, n)
    g = lambda n: a["L0_attn_" + n]
    w, v = [], []
    for l in range(4):
        w.append(np.concatenate([diagonal(g("Wk")[l]), diagonal(g("Wq")[l]), diagonal(g("Wv")[l]),
                                 diagonal(g("Wo")[l]), twice(g("W1")[l]), second(g("W2")[l])], axis=1))
        cols = [g("g1")[l], g("b1")[l], g("bo")[l], g("g2")[l], g("b2")[l]]
        v.append(np.concatenate([twice(np.stack(cols, axis=1)), g("bf1")[l].reshape(2, P).T,
                                 twice(g("bf2")[l][:, None])], axis=1))
    t["lin_w"], t["lin_v"] = np.stack(w), np.stack(v)
    g = lambda n: a["L0_ffn_" + n]
    up = g("W1").transpose(1, 0, 2).reshape(C, EXP * P)
    down = g("W2").transpose(1, 0, 2).reshape(P, EXP * C)
    t["moe_w"] = np.concatenate([diagonal(g("Wr")), down], axis=1)
    t["moe_w1"] = twice(up)
    t["moe_v"] = np.concatenate([twice(np.stack([g("gamma"), g("beta")], axis=1)), g("b1").T], axis=1)
    t["moe_br"] = np.tile(g("br"), (TT, 2))
    t["moe_b2"] = np.tile(diagonal(g("b2")), (3, 1))
    return t


def kernel(**inputs):
    import concourse.bacc as _bacc
    from concourse.bass_utils import run_bass_kernel_spmd as _run

    nc = _bacc.Bacc("TRN2", target_bir_lowering=False, num_devices=1)
    arrays, args = {}, {}
    for name, a in {**constants(), **laid_out(inputs)}.items():
        a = np.ascontiguousarray(a)
        arrays[f"in_{name}"] = a
        args[name] = nc.dram_tensor(f"in_{name}", a.shape, mybir.dt.from_np(a.dtype), kind="ExternalInput").ap()
    out = nc.dram_tensor("out_0", (B, SEQ, C), F32, kind="ExternalOutput").ap()
    vit_tower(nc, args, out)
    return _run(nc, [arrays], core_ids=[0]).results[0]["out_0"]
```
